# Optimizing a Trainium2 kernel written in Bass

```python
import numpy as np
import jax
import jax.numpy as jnp

def _softmax(x, axis=-1):
    return jax.nn.softmax(x, axis=axis)

def _gelu(x):
    return jax.nn.gelu(x, approximate=True)

def _silu(x):
    return jax.nn.silu(x)

def _sigmoid(x):
    return jax.nn.sigmoid(x)

def _layernorm(x, axis=-1, eps=1e-05):
    m = jnp.mean(x, axis=axis, keepdims=True)
    v = jnp.var(x, axis=axis, keepdims=True)
    return (x - m) / jnp.sqrt(v + eps)

def _scatter_add(tgt, idx, src, axis=0):
    return tgt.at[idx].add(src)

def _segment_sum(src, seg, n):
    return jax.ops.segment_sum(src, seg, n)
kernel_name = 'mk_seq_postln_d1_jaxref_r4_702da6'

def setup_inputs(seed: int=0):
    np.random.seed(seed)
    _w = jnp.asarray

    def _L0_attn_setup():
        import jax, jax.numpy as jnp
        import numpy as np
        B, T, D = (4, 512, 256)

        def ste_sign(x):
            return jax.lax.stop_gradient(jnp.sign(x) - x) + x
        key = jax.random.key(seed)
        kx, kq, kk, kv = jax.random.split(key, 4)
        return {'x': jax.random.normal(kx, (B, T, D), dtype=jnp.float32), 'bv_q': jax.random.normal(kq, (D,), dtype=jnp.float32) * 0.02, 'bv_k': jax.random.normal(kk, (D,), dtype=jnp.float32) * 0.02, 'bv_v': jax.random.normal(kv, (D,), dtype=jnp.float32) * 0.02}
    _L0_attn_in = _L0_attn_setup()

    def _L0_ffn_setup():
        import math
        import jax, jax.numpy as jnp
        import numpy as np
        CAPACITY_FACTOR = 1.25
        key = jax.random.key(seed)
        ks = jax.random.split(key, 5)
        B, S, H, F, E = (4, 1024, 256, 256, 32)
        scale_in = 1.0 / math.sqrt(H)
        scale_mid = 1.0 / math.sqrt(F)
        return {'x': jax.random.normal(ks[0], (B, S, H), dtype=jnp.float32), 'w_router': jax.random.normal(ks[1], (H, E), dtype=jnp.float32) * scale_in, 'w_gate': jax.random.normal(ks[2], (E, H, F), dtype=jnp.float32) * scale_in, 'w_up': jax.random.normal(ks[3], (E, H, F), dtype=jnp.float32) * scale_in, 'w_down': jax.random.normal(ks[4], (E, F, H), dtype=jnp.float32) * scale_mid}
    _L0_ffn_in = _L0_ffn_setup()
    _d = {'L0_attn_x': _L0_attn_in['x'], 'L0_attn_bv_q': _L0_attn_in['bv_q'], 'L0_attn_bv_k': _L0_attn_in['bv_k'], 'L0_attn_bv_v': _L0_attn_in['bv_v'], 'L0_ffn_w_router': _L0_ffn_in['w_router'], 'L0_ffn_w_gate': _L0_ffn_in['w_gate'], 'L0_ffn_w_up': _L0_ffn_in['w_up'], 'L0_ffn_w_down': _L0_ffn_in['w_down']}
    _x0 = _d['L0_attn_x']
    _d['L0_attn_x'] = jax.random.normal(jax.random.fold_in(jax.random.key(seed), 1), (4, 2048, 256), dtype=_x0.dtype)
    del _x0
    return _d

def reference(L0_attn_x, L0_attn_bv_q, L0_attn_bv_k, L0_attn_bv_v, L0_ffn_w_router, L0_ffn_w_gate, L0_ffn_w_up, L0_ffn_w_down):

    def _L0_attn_ref(x, bv_q, bv_k, bv_v):
        import jax, jax.numpy as jnp
        import numpy as np
        B, T, D = (4, 512, 256)

        def ste_sign(x):
            return jax.lax.stop_gradient(jnp.sign(x) - x) + x
        d = x.shape[-1]
        scale = d ** (-0.5)
        bq = ste_sign(bv_q)
        bk = ste_sign(bv_k)
        bv = ste_sign(bv_v)
        Q = ste_sign(x * bq)
        K = ste_sign(x * bk)
        V = x * bv
        scores = jnp.einsum('btd,bsd->bts', Q, K) * scale
        t = x.shape[1]
        causal = jnp.tril(jnp.ones((t, t), dtype=bool))
        scores = jnp.where(causal, scores, -jnp.inf)
        attn = jax.nn.sigmoid(scores * 4.0)
        attn = jnp.where(causal, attn, 0.0)
        return jnp.einsum('bts,bsd->btd', attn, V)

    def _L0_ffn_ref(x, w_router, w_gate, w_up, w_down):
        import math
        import jax, jax.numpy as jnp
        import numpy as np
        CAPACITY_FACTOR = 1.25
        B, S, H = x.shape
        E = w_gate.shape[0]
        T = B * S
        C = int(math.ceil(CAPACITY_FACTOR * T / E))
        xt = x.reshape(T, H)
        logits = xt @ w_router
        probs = jax.nn.softmax(logits, axis=-1)
        top1 = jnp.argmax(probs, axis=-1)
        gate = jnp.take_along_axis(probs, top1[:, None], axis=1)[:, 0]
        onehot = jax.nn.one_hot(top1, E, dtype=jnp.int32)
        pos = jnp.cumsum(onehot, axis=0)[jnp.arange(T), top1] - 1
        accepted = pos < C
        slot = jnp.where(accepted, top1 * C + pos, E * C)
        buf = jnp.zeros((E * C + 1, H), dtype=x.dtype).at[slot].set(xt)
        buf = buf[:E * C].reshape(E, C, H)
        g = jnp.einsum('ech,ehf->ecf', buf, w_gate)
        u = jnp.einsum('ech,ehf->ecf', buf, w_up)
        y = jnp.einsum('ecf,efh->ech', jax.nn.silu(g) * u, w_down)
        out_tok = y.reshape(E * C, H)[jnp.clip(slot, 0, E * C - 1)]
        out_tok = jnp.where(accepted[:, None], out_tok * gate[:, None], 0.0)
        return (xt + out_tok).reshape(B, S, H)
    x = L0_attn_x
    x = _layernorm(x + _L0_attn_ref(x, L0_attn_bv_q, L0_attn_bv_k, L0_attn_bv_v), axis=-1)
    x = _layernorm(x + _L0_ffn_ref(x, L0_ffn_w_router, L0_ffn_w_gate, L0_ffn_w_up, L0_ffn_w_down), axis=-1)
    return x

_drawn_inputs = setup_inputs


def setup_inputs(seed=0):
    import zlib

    import numpy as np

    out = dict(_drawn_inputs(seed))
    spreads = {}
    factors = {}
    for name, (base, spread) in spreads.items():
        noise = np.random.default_rng([zlib.crc32(name.encode()), seed]).standard_normal(out[name].shape)
        drawn = base * np.exp(spread * noise) if base else spread * noise
        out[name] = jnp.asarray(drawn.astype(out[name].dtype))
    for name, factor in factors.items():
        out[name] = (out[name] * factor).astype(out[name].dtype)
    return out
```

```python
from contextlib import ExitStack

import numpy as np

import concourse.bass as bass
from concourse import mybir

ALU = mybir.AluOpType
ACT = mybir.ActivationFunctionType
AX_X = mybir.AxisListType.X
F32 = mybir.dt.float32
F32R = mybir.dt.float32r
BF16 = mybir.dt.bfloat16
U32 = mybir.dt.uint32

P = 128
EPS = 1e-5
MASKED = -30000.0
SKIP = 65536.0

GT = 4
GQ = GT * P
RING = 4

TAIL_BACK = {3: 2, 0: 11, 1: 20, 2: 29}
TAIL_TURN = {g: s + 3 for g, s in TAIL_BACK.items()}
TAIL_ROUTE = {g: s + 5 for g, s in TAIL_BACK.items()}
TAIL_COUNT = {g: s + 6 for g, s in TAIL_BACK.items()}
TAIL_SCALE = {3: 1, 0: 7, 1: 15, 2: 27}
PREP = {2: 4, 3: 13, 0: 37, 1: 39}
PREP_SIGN = {2: 4, 3: 13, 0: 36, 1: 38}


def bass_postln_attn_moe_kernel(nc, x, bv_q, bv_k, bv_v, w_router, w_gate, w_up, w_down, out):
    B, T, D = x.shape
    E, _, F = w_gate.shape
    NT = B * T // P
    NG = T // GQ
    DC, FC = D // P, F // P
    N_TOK = B * T
    CAP = -(-5 * N_TOK // (4 * E))
    ROW = D + 2
    CT = -(-CAP // P)
    CFULL = CAP // P
    CREST = CAP - CFULL * P
    SLOTS = E * CAP
    assert NG == 4 and DC == 2 and FC == 2 and NT == 64 and CREST > 0 and E == 32
    STEPS = [(g, j) for g in range(NG) for j in range(GT * g + GT)]
    OFF = [0, 4, 12, 24]
    NS = len(STEPS)
    END = [OFF[g] + GT * g + GT for g in range(NG)]
    SLOT_W = 10
    SLOT_X = 5
    assert (E - 2) % SLOT_W == 0

    x_rows = x.rearrange("b t d -> (b t) d")
    out_rows = out.rearrange("b t d -> (b t) d")
    buf = nc.dram_tensor("expert_rows", [SLOTS, ROW], F32)
    buf_rows = buf.ap()

    with ExitStack() as ctx:
        def sb(name, shape, dt):
            return ctx.enter_context(nc.sbuf_tensor(name, shape, dt))

        def sem(name):
            return ctx.enter_context(nc.semaphore(name))

        ps = ctx.enter_context(nc.psum_tensor("ps", [P, 8, 512], F32))
        ident = sb("ident", [P, P], F32)
        identb = sb("identb", [P, P], BF16)
        tri = sb("tri", [P, P], BF16)
        onesb = sb("onesb", [P, P], BF16)
        maskb = sb("maskb", [P, P], BF16)
        iota_e = sb("iota_e", [P, GT, E], F32)
        tok = sb("tok", [P, GT], F32)
        mhalf = sb("mhalf", [P, GT], F32)
        bvec = sb("bvec", [P, 3, DC], F32)
        bsgn = sb("bsgn", [P, 3, DC], F32)
        qk_sgn = sb("qk_sgn", [P, DC], F32)
        w_r = sb("w_r", [P, DC, E], F32)
        zero = sb("zero", [P, 4 * ROW], F32)

        xall = sb("xall", [P, NT, D], F32)
        v_hl = sb("v_hl", [P, 2, T // P, D], F32R)
        sgn = sb("sgn", [P, GT, D], BF16)
        q_t = sb("q_t", [P, DC, T], BF16)
        k_t = sb("k_t", [P, DC, T], BF16)
        a_ring = sb("a_ring", [P, RING, GQ], F32)
        hl_ring = sb("hl_ring", [P, 2, RING, GQ], F32R)
        o_t = sb("o_t", [P, 2, DC, GQ], F32)
        res = sb("res", [P, GT, D], F32)
        stats = sb("stats", [P, GT, 6], F32)
        mv = sb("mv", [P, GT, 2], F32)
        small = sb("small", [P, 8, GT], F32)
        xrow = sb("xrow", [P, 2, GT, ROW], F32)
        alone = sb("alone", [P, 2, GT, D], F32)
        x1_t = sb("x1_t", [P, DC, GQ], F32)
        lg = sb("lg", [P, GT, E], F32)
        top = sb("top", [P, GT, 8], F32)
        topi = sb("topi", [P, GT, 8], U32)
        topf = sb("topf", [P, GT], F32)
        hot = sb("hot", [P, GT, E], BF16)
        below = sb("below", [P, GT, E], F32)
        sg = sb("sg", [P, 2, GT, E], F32)
        rneg = sb("rneg", [P, GT, E], F32)
        pm = sb("pm", [P, GT, E], F32)
        hots = sb("hots", [P, E], F32)
        seen = sb("seen", [P, E], BF16)
        rt = sb("rt", [P, 6, GT], F32)
        slot = sb("slot", [P, 2, GT], U32)

        raw = xall[:, 0:6 * SLOT_W, :].rearrange("p (s k) f -> p s k f", k=6)
        v_flat = v_hl[:, :, :, :].rearrange("p a t d -> p (a t d)")
        WN = 6 * F
        w_h = v_flat[:, 0:2 * WN].rearrange("p (s k f) -> p s k f", s=2, f=F)
        w_l = v_flat[:, 2 * WN:4 * WN].rearrange("p (s k f) -> p s k f", s=2, f=F)
        h_l = v_flat[:, 4 * WN:4 * WN + 2 * FC * CAP].rearrange("p (s k t) -> p s k t", s=2, t=CAP)
        r_flat = hl_ring[:, :, :, :].rearrange("p a r t -> p (a r t)")
        XN = DC * CAP
        x_h = r_flat[:, 0:2 * XN].rearrange("p (s k t) -> p s k t", s=2, t=CAP)
        x_l = r_flat[:, 2 * XN:4 * XN].rearrange("p (s k t) -> p s k t", s=2, t=CAP)
        h_h = r_flat[:, 4 * XN:4 * XN + 2 * FC * CAP].rearrange("p (s k t) -> p s k t", s=2, t=CAP)
        xs = sb("xs", [P, SLOT_X, CT, ROW], F32)
        a_flat = a_ring[:, :, :].rearrange("p r t -> p (r t)")
        act_s, act_t, act_h = (a_flat[:, n * FC * CAP:(n + 1) * FC * CAP].rearrange("p (k t) -> p k t", k=FC)
                               for n in range(3))
        z = o_t[:, :, :, :].rearrange("p a c t -> p (a c t)")[:, 0:CT * D].rearrange("p (t d) -> p t d", d=D)
        zst = sb("zst", [P, CT, 6], F32)
        zmv = sb("zmv", [P, 2, CT, 2], F32)
        zrs = sb("zrs", [P, 2, 2, CT], F32)
        idt = sb("idt", [P, 2, CT], F32)
        ids = sb("ids", [P, 2, CT], U32)
        o_s = alone[:, :, 0:CT, :]

        x_in = [sem(f"x_in{q}") for q in range(NG)]
        small_in = sem("small_in")
        zero_set = sem("zero_set")
        zero_out = sem("zero_out")
        consts = sem("consts")
        consts_step = sem("consts_step")
        bsgn_ready = sem("bsgn_ready")
        qksgn_ready = sem("qksgn_ready")
        sgn_ready = sem("sgn_ready")
        vh_ready = sem("vh_ready")
        v_ready = sem("v_ready")
        sgn_turned = sem("sgn_turned")
        qt_ready = sem("qt_ready")
        kt_ready = sem("kt_ready")
        scores_ready = sem("scores_ready")
        a_ready = sem("a_ready")
        ah_ready = sem("ah_ready")
        al_ready = sem("al_ready")
        pv_done = sem("pv_done")
        ot_ready = sem("ot_ready")
        back_done = sem("back_done")
        res_ready = sem("res_ready")
        stats_step = sem("stats_step")
        mv_ready = sem("mv_ready")
        rstd_step = sem("rstd_step")
        x1_ready = sem("x1_ready")
        x1_turned = sem("x1_turned")
        x1t_ready = sem("x1t_ready")
        logits_done = sem("logits_done")
        lg_ready = sem("lg_ready")
        route_step = sem("route_step")
        hot_ready = sem("hot_ready")
        below_ready = sem("below_ready")
        sg_ready = sem("sg_ready")
        counts_done = sem("counts_done")
        pos_read = sem("pos_read")
        seen_ready = sem("seen_ready")
        gate_step = sem("gate_step")
        gate_ready = sem("gate_ready")
        slot_ready = sem("slot_ready")
        tok_step = sem("tok_step")
        alone_ready = sem("alone_ready")
        alone_out = [sem(f"alone_out{i}") for i in range(2)]
        scattered = [sem(f"scattered{i}") for i in range(2)]

        raw_in = [sem(f"raw_in{i}") for i in range(SLOT_W)]
        xs_clear = sem("xs_clear")
        xs_in = [sem(f"xs_in{i}") for i in range(SLOT_X)]
        xs_turned = sem("xs_turned")
        xh_ready = sem("xh_ready")
        xl_ready = sem("xl_ready")
        whgu_ready = sem("whgu_ready")
        whd_ready = sem("whd_ready")
        wlgu_ready = sem("wlgu_ready")
        wld_ready = sem("wld_ready")
        gu_done = sem("gu_done")
        sig_ready = sem("sig_ready")
        hid_step = sem("hid_step")
        hh_ready = sem("hh_ready")
        hl_ready = sem("hl_ready")
        y_done = sem("y_done")
        z_step = sem("z_step")
        zst_step = sem("zst_step")
        zmv_clear = sem("zmv_clear")
        zmv_ready = sem("zmv_ready")
        zr_step = sem("zr_step")
        zrs_ready = sem("zrs_ready")
        ids_step = sem("ids_step")
        ids_ready = sem("ids_ready")
        os_ready = sem("os_ready")
        os_out = [sem(f"os_out{i}") for i in range(2)]

        def atleast(eng, s, value, settle=False):
            if isinstance(value, int) and value <= 0:
                return
            if settle and not isinstance(value, int):
                value = eng.to_reg(value)
                eng.wait_ge(consts, 8)
            eng.wait_ge(s, value)

        block = ctx.enter_context(nc.Block())
        M0, M1 = 6, 7

        def cols(k):
            g, j = STEPS[k]
            return g, j, max(0, j - GT * g) * P

        @block.sync
        def _(sp):
            def load_x(b, q):
                src = x[b, q * GQ:(q + 1) * GQ, :].rearrange("(i p) d -> p i d", p=P)
                sp.dma_start(xall[:, bass.ds(b * (T // P) + GT * q, GT), :], src).then_inc(x_in[q], 16)

            load_x(0, 0)
            for n, v in enumerate((bv_q, bv_k, bv_v)):
                sp.dma_start(bvec[:, n, :], v.rearrange("(c p) -> p c", p=P),
                             allow_slow_non_contiguous=True).then_inc(small_in, 16)
            sp.dma_start(w_r[:, :, :], w_router.rearrange("(c p) e -> p c e", p=P)).then_inc(small_in, 16)
            for q in range(1, NG):
                load_x(0, q)
            sp.wait_ge(zero_set, 1)
            per = SLOTS // (P * 4)
            zrows = buf_rows.rearrange("(n p r) w -> n p (r w)", p=P, r=4)
            for n in range(per):
                sp.dma_start(zrows[n], zero[:, :]).then_inc(zero_out, 16)

            def store_alone(G, par):
                atleast(sp, alone_ready, 4 * G + 4)
                dst = out_rows[bass.ds(G * GQ, GQ), :].rearrange("(i p) d -> p i d", p=P)
                sp.dma_start(dst, alone[:, par, :, :]).then_inc(alone_out[par], 16)

            with sp.Fori(1, B) as b:
                for q in range(NG):
                    sp.wait_ge(v_ready, (b - 1) * NG + q + 1)
                    sp.wait_ge(sgn_ready, (b - 1) * NG + q + 1)
                    load_x(b, q)
                    store_alone((b - 1) * NG + q, q % 2)

            def load_raw(e, s):
                for n, w in enumerate((w_gate, w_up, w_down)):
                    sp.dma_start(raw[:, s, 2 * n:2 * n + 2, :],
                                 w[e].rearrange("(c p) f -> p c f", p=P)).then_inc(raw_in[s], 16)

            def load_xs(e, s):
                rows = buf_rows[bass.ds(e * CAP, CAP), :]
                sp.dma_start(xs[:, s, 0:CFULL, :],
                             rows[0:CFULL * P, :].rearrange("(i p) w -> p i w", p=P)).then_inc(xs_in[s], 16)
                sp.dma_start(xs[0:CREST, s, CFULL, :], rows[CFULL * P:CAP, :]).then_inc(xs_in[s], 16)

            last = (B - 1) * NG
            for s in range(SLOT_W):
                sp.wait_ge(res_ready, (6 * s + 5) // GT + 1)
                if (6 * s + 5) // GT >= last:
                    sp.wait_ge(v_ready, last + NG)
                load_raw(s, s)
                if s >= SLOT_W - 2:
                    for q in (2 * (s - SLOT_W + 2), 2 * (s - SLOT_W + 2) + 1):
                        store_alone(last + q, q % 2)
            for par in range(2):
                sp.wait_ge(scattered[par], 16 * GT * B * NG // 2)
            sp.wait_ge(xs_clear, 1)
            for e in range(SLOT_X):
                load_xs(e, e)

            def refill(R, i):
                e = R * SLOT_W + i
                if not (isinstance(e, int) and e + SLOT_X >= E):
                    sp.wait_ge(z_step, (e + 1) * CT)
                    sp.wait_ge(ids_ready, e + 1)
                    load_xs(e + SLOT_X, i % SLOT_X)
                if not (isinstance(e, int) and e + SLOT_W >= E):
                    sp.wait_ge(whgu_ready, e + 1)
                    sp.wait_ge(whd_ready, e + 1)
                    sp.wait_ge(wlgu_ready, e + 1)
                    sp.wait_ge(wld_ready, e + 1)
                    load_raw(e + SLOT_W, i % SLOT_W)

            with sp.Fori(0, (E - SLOT_W) // SLOT_W) as R:
                for i in range(SLOT_W):
                    refill(R, i)
            for e in range((E - SLOT_W) // SLOT_W * SLOT_W, E):
                refill(e // SLOT_W, e % SLOT_W)
            for par in range(2):
                sp.wait_ge(alone_out[par], 16 * B * NG // 2)

        @block.gpsimd
        def _(pool):
            g_ = nc.gpsimd
            g_.memset(zero[:, :], 0.0).then_inc(zero_set, 1)
            g_.memset(ident[:, :], 0.0).then_inc(consts_step, 1)
            g_.memset(identb[:, :], 0.0).then_inc(consts_step, 1)
            g_.memset(tri[:, :], 1.0).then_inc(consts_step, 1)
            g_.memset(maskb[:, :], 0.0).then_inc(consts_step, 1)
            g_.memset(onesb[:, :], 1.0).then_inc(consts, 1)
            g_.memset(mhalf[:, :], -0.5).then_inc(consts, 1)
            pool.wait_ge(consts_step, 4)
            for m in (ident, identb):
                g_.affine_select(out=m[:, :], in_=m[:, :], compare_op=ALU.not_equal, fill=1.0, base=0,
                                 pattern=[[-1, P]], channel_multiplier=1).then_inc(consts, 1)
            g_.affine_select(out=tri[:, :], in_=tri[:, :], compare_op=ALU.is_ge, fill=0.0, base=0,
                             pattern=[[1, P]], channel_multiplier=-1).then_inc(consts, 1)
            g_.affine_select(out=maskb[:, :], in_=maskb[:, :], compare_op=ALU.is_ge, fill=MASKED, base=0,
                             pattern=[[1, P]], channel_multiplier=-1).then_inc(consts, 1)
            g_.iota(iota_e[:, :, :], pattern=[[0, GT], [1, E]], base=0, channel_multiplier=0,
                    allow_small_or_imprecise_dtypes=True).then_inc(consts, 1)
            g_.iota(tok[:, :], pattern=[[P, GT]], base=1, channel_multiplier=1,
                    allow_small_or_imprecise_dtypes=True).then_inc(consts, 1)

            def split_v(b, q):
                sl = slice(GT * q, GT * q + GT)
                src = xall[:, bass.ds(b * (T // P) + GT * q, GT), :]
                atleast(pool, x_in[q], (b + 1) * 16, settle=True)
                atleast(pool, pv_done, (b - 1) * NS + OFF[3] + GT * q + GT, settle=True)
                g_.tensor_copy(v_hl[:, 0, sl, :], src).then_inc(vh_ready, 1)
                atleast(pool, vh_ready, b * NG + q + 1, settle=True)
                g_.tensor_tensor(v_hl[:, 1, sl, :], src, v_hl[:, 0, sl, :].bitcast(F32),
                                 ALU.subtract).then_inc(v_ready, 1)

            RN = 6

            def rstd(G, par):
                atleast(pool, mv_ready, (G + 1) * GT, settle=True)
                atleast(pool, alone_ready, G * GT, settle=True)
                base = G * RN
                atleast(pool, x1_ready, G * GT, settle=True)
                var = mv[:, :, 1]
                g_.tensor_scalar(small[:, 0, :], var, EPS, None, ALU.add).then_inc(rstd_step, 1)
                atleast(pool, rstd_step, base + 1, settle=True)
                g_.tensor_tensor(small[:, 1, :], small[:, 0, :], mhalf[:, :], ALU.pow).then_inc(rstd_step, 1)
                atleast(pool, rstd_step, base + 2, settle=True)
                g_.tensor_tensor(small[:, 2, :], var, small[:, 1, :], ALU.mult).then_inc(rstd_step, 1)
                atleast(pool, rstd_step, base + 3, settle=True)
                g_.tensor_tensor(small[:, 3, :], small[:, 2, :], small[:, 1, :], ALU.mult).then_inc(rstd_step, 1)
                atleast(pool, rstd_step, base + 4, settle=True)
                g_.tensor_scalar(small[:, 4, :], small[:, 3, :], EPS / 4, None, ALU.add).then_inc(rstd_step, 1)
                atleast(pool, rstd_step, base + 5, settle=True)
                g_.tensor_tensor(small[:, 5, :], small[:, 4, :], mhalf[:, :], ALU.pow).then_inc(rstd_step, 1)

            def rows_alone(G, half, par):
                atleast(pool, rstd_step, G * RN + RN, settle=True)
                atleast(pool, x1_ready, (G + 1) * GT, settle=True)
                atleast(pool, alone_out[par], half * 16, settle=True)
                for i in range(GT):
                    g_.tensor_scalar(alone[:, par, i, :], xrow[:, par, i, 0:D], small[:, 5, i:i + 1], None,
                                     ALU.mult).then_inc(alone_ready, 1)
                g_.tensor_copy(xrow[:, par, :, D + 1], tok[:, :]).then_inc(tok_step, 1)
                atleast(pool, tok_step, G * 2 + 1, settle=True)
                g_.tensor_scalar(tok[:, :], tok[:, :], float(GQ), None, ALU.add).then_inc(tok_step, 1)
                atleast(pool, tok_step, G * 2 + 2, settle=True)

            def scatter(G, par):
                atleast(pool, gate_ready, G + 1, settle=True)
                atleast(pool, slot_ready, G + 1, settle=True)
                for i in range(GT):
                    g_.indirect_dma_start(
                        out=buf_rows, out_offset=bass.IndirectOffsetOnAxis(ap=slot[:, par, i:i + 1], axis=0),
                        in_=xrow[:, par, i, :], in_offset=None, bounds_check=SLOTS - 1,
                        oob_is_err=False).then_inc(scattered[par], 16)

            def batch(b, first):
                n = b * NG
                if not first:
                    rstd(n - 1, 1)
                    rows_alone(n - 1, 2 * b - 1, 1)
                split_v(b, 2)
                if not first:
                    scatter(n - 1, 1)
                rstd(n, 0)
                rows_alone(n, 2 * b, 0)
                split_v(b, 3)
                scatter(n, 0)
                rstd(n + 1, 1)
                rows_alone(n + 1, 2 * b, 1)
                scatter(n + 1, 1)
                rstd(n + 2, 0)
                rows_alone(n + 2, 2 * b + 1, 0)

            split_v(0, 0)
            split_v(0, 1)
            pool.wait_ge(consts, 8)
            atleast(pool, zero_out, 16 * (SLOTS // (P * 4)), settle=True)
            batch(0, True)
            split_v(1, 0)
            scatter(2, 0)
            split_v(1, 1)
            with pool.Fori(1, B - 1) as b:
                batch(b, False)
                split_v(b + 1, 0)
                scatter(b * NG + 2, 0)
                split_v(b + 1, 1)
            batch(B - 1, False)
            last = (B - 1) * NG
            scatter(last + 2, 0)
            rstd(last + 3, 1)
            rows_alone(last + 3, 2 * B - 1, 1)
            scatter(last + 3, 1)

            g_.memset(xs[:, :, :, :], 0.0).then_inc(xs_clear, 1)
            atleast(pool, pv_done, B * NS, settle=True)

            def low_gu(R, i):
                e, s, p = R * SLOT_W + i, i % SLOT_W, i % 2
                atleast(pool, whgu_ready, e + 1, settle=True)
                atleast(pool, gu_done, 2 * (e - 1), settle=True)
                g_.tensor_tensor(w_l[:, p, 0:4, :], raw[:, s, 0:4, :], w_h[:, p, 0:4, :].bitcast(F32),
                                 ALU.subtract).then_inc(wlgu_ready, 1)

            def numbers(R, i):
                e, p = R * SLOT_W + i, i % 2
                atleast(pool, xs_in[i % SLOT_X], 32 * (R * (SLOT_W // SLOT_X) + i // SLOT_X + 1), settle=True)
                v = xs[:, i % SLOT_X, :, D + 1]
                atleast(pool, os_out[p], 16 * CT * (R * (SLOT_W // 2) + i // 2), settle=True)
                base = e * 2
                g_.tensor_scalar(idt[:, 0, :], v, 0.5, SKIP, ALU.is_lt, ALU.mult).then_inc(ids_step, 1)
                atleast(pool, ids_step, base + 1, settle=True)
                g_.tensor_tensor(idt[:, 1, :], idt[:, 0, :], v, ALU.add).then_inc(ids_step, 1)
                atleast(pool, ids_step, base + 2, settle=True)
                g_.tensor_scalar(ids[:, p, :], idt[:, 1, :], -1.0, None, ALU.add).then_inc(ids_ready, 1)
                atleast(pool, ids_ready, e + 1, settle=True)

            def second_rstd(R, i):
                e, p = R * SLOT_W + i, i % 2
                atleast(pool, zmv_ready, (e + 1) * CT, settle=True)
                g_.tensor_scalar(zrs[:, p, 0, :], zmv[:, p, :, 1], EPS / 4, None, ALU.add).then_inc(zr_step, 1)
                atleast(pool, zr_step, e + 1, settle=True)
                g_.tensor_tensor(zrs[:, p, 1, :], zrs[:, p, 0, :], mhalf[:, 0:CT], ALU.pow)\
                    .then_inc(zrs_ready, 1)

            def store(R, i):
                e, p = R * SLOT_W + i, i % 2
                atleast(pool, os_ready, (e + 1) * CT, settle=True)
                for t in range(CT):
                    n = P if t < CFULL else CREST
                    g_.indirect_dma_start(
                        out=out_rows, out_offset=bass.IndirectOffsetOnAxis(ap=ids[0:n, p, t:t + 1], axis=0),
                        in_=o_s[0:n, p, t, :], in_offset=None, bounds_check=N_TOK - 1,
                        oob_is_err=False).then_inc(os_out[p], 16)

            for par in range(2):
                atleast(pool, alone_out[par], 16 * B * NG // 2, settle=True)
            low_gu(0, 0)
            numbers(0, 0)
            low_gu(0, 1)

            def expert(R, i):
                second_rstd(R, i - 1)
                store(R, i - 1)
                low_gu(R, i + 1)
                numbers(R, i)

            with pool.Fori(0, (E - 2) // SLOT_W) as R:
                for i in range(1, SLOT_W + 1):
                    expert(R, i)
            RL = (E - 2) // SLOT_W
            second_rstd(RL, 0)
            store(RL, 0)
            numbers(RL, 1)
            second_rstd(RL, 1)
            store(RL, 1)
            for par in range(2):
                atleast(pool, os_out[par], 16 * CT * E // 2, settle=True)

        @block.scalar
        def _(act):
            s_ = nc.scalar
            act.wait_ge(small_in, 64)
            s_.activation(bsgn[:, :, :], bvec[:, :, :], ACT.Sign).then_inc(bsgn_ready, 1)
            act.wait_ge(bsgn_ready, 1)

            def signs(b, q):
                act.wait_ge(x_in[q], (b + 1) * 16)
                atleast(act, sgn_turned, b * NG + q)
                s_.activation(sgn[:, :, :], xall[:, bass.ds(b * (T // P) + GT * q, GT), :], ACT.Sign)\
                    .then_inc(sgn_ready, 1)

            def weights(b, k):
                g, j, lo = cols(k)
                n = b * NS + k
                act.wait_ge(scores_ready, n + 1)
                atleast(act, al_ready, n - RING + 1)
                atleast(act, pv_done, n - RING + 1)
                r = k % RING
                s_.activation(a_ring[:, r, lo:GQ], ps[:, k % 2, lo:GQ], ACT.Sigmoid, scale=0.25)\
                    .then_inc(a_ready, 1)
                s_.activation(hl_ring[:, 0, r, lo:GQ], ps[:, k % 2, lo:GQ], ACT.Sigmoid, scale=0.25)\
                    .then_inc(ah_ready, 1)

            def scale_out(b, g):
                G = b * NG + g
                act.wait_ge(pv_done, b * NS + END[g])
                atleast(act, back_done, G - 1)
                for c in range(DC):
                    s_.activation(o_t[:, g % 2, c, :], ps[:, 2 + 2 * (g % 2) + c, :], ACT.Copy,
                                  scale=bsgn[:, 2, c:c + 1]).then_inc(ot_ready, 1)

            def copy_x1t(G):
                act.wait_ge(x1_turned, G + 1)
                atleast(act, logits_done, G)
                for c in range(DC):
                    s_.activation(x1_t[:, c, :], ps[:, M0 + c, :], ACT.Copy).then_inc(x1t_ready, 1)

            def gates(G):
                act.wait_ge(below_ready, G + 1)
                atleast(act, gate_ready, G)
                s_.activation(sg[:, 0, :, :], below[:, :, :], ACT.Sigmoid).then_inc(sg_ready, 1)
                s_.activation(sg[:, 1, :, :], below[:, :, :], ACT.Sigmoid, scale=-1.0).then_inc(sg_ready, 1)

            def batch(b, first, last):
                for k in range(NS):
                    weights(b, k)
                    for g in range(NG):
                        bb = b - 1 if g == 3 else b
                        if g == 3 and first:
                            continue
                        if k == TAIL_SCALE[g]:
                            scale_out(bb, g)
                        if k == TAIL_TURN[g] + 2:
                            copy_x1t(bb * NG + g)
                        if k == TAIL_COUNT[g] + 1:
                            gates(bb * NG + g)
                    for q in range(NG):
                        if k == PREP_SIGN[q]:
                            if q < 2 and last:
                                continue
                            signs(b + 1 if q < 2 else b, q)

            signs(0, 0)
            signs(0, 1)
            batch(0, True, False)
            with act.Fori(1, B - 1) as b:
                batch(b, False, False)
            batch(B - 1, False, True)
            scale_out(B - 1, 3)
            copy_x1t(B * NG - 1)
            gates(B * NG - 1)

            def high_gu(R, i):
                e, s, p = R * SLOT_W + i, i % SLOT_W, i % 2
                act.wait_ge(raw_in[s], 48 * (R + i // SLOT_W + 1))
                atleast(act, gu_done, 2 * (e - 1))
                atleast(act, wlgu_ready, e - 1)
                s_.activation(w_h[:, p, 0:4, :], raw[:, s, 0:4, :], ACT.Copy).then_inc(whgu_ready, 1)

            def high_d(R, i):
                e, s, p = R * SLOT_W + i, i % SLOT_W, i % 2
                atleast(act, y_done, (e - 1) * CT)
                atleast(act, wld_ready, e - 1)
                act.wait_ge(raw_in[s], 48 * (R + i // SLOT_W + 1))
                s_.activation(w_h[:, p, 4:6, :], raw[:, s, 4:6, :], ACT.Copy).then_inc(whd_ready, 1)

            def high_x(R, i):
                e, p = R * SLOT_W + i, i % 2
                act.wait_ge(xs_turned, e + 1)
                atleast(act, gu_done, 2 * (e - 1))
                atleast(act, xl_ready, e - 1)
                s_.activation(x_h[:, p, :, :], ps[:, 0:DC, 0:CAP], ACT.Copy).then_inc(xh_ready, 1)

            def gate_sigmoid(R, i, f):
                e = R * SLOT_W + i
                act.wait_ge(gu_done, 2 * e + f + 1)
                atleast(act, hid_step, 4 * e + 2 * f - 3)
                s_.activation(act_s[:, f, :], ps[:, 2 + 2 * f, 0:CAP], ACT.Sigmoid).then_inc(sig_ready, 1)

            def high_hidden(R, i, f):
                e, p = R * SLOT_W + i, i % 2
                act.wait_ge(hid_step, 4 * e + 2 * f + 2)
                atleast(act, y_done, (e - 1) * CT)
                s_.activation(h_h[:, p, f, :], act_h[:, f, :], ACT.Copy).then_inc(hh_ready, 1)

            def expert(R, i, last=False):
                if not last:
                    high_gu(R, i + 1)
                gate_sigmoid(R, i, 0)
                high_hidden(R, i, 0)
                if not last:
                    high_d(R, i + 1)
                    high_x(R, i + 1)
                gate_sigmoid(R, i, 1)
                high_hidden(R, i, 1)

            act.wait_ge(pv_done, B * NS)
            high_gu(0, 0)
            high_d(0, 0)
            high_x(0, 0)
            expert(0, 0)
            with act.Fori(0, (E - 2) // SLOT_W) as R:
                for i in range(1, SLOT_W + 1):
                    expert(R, i)
            expert((E - 2) // SLOT_W, 1, last=True)

        @block.tensor
        def _(pe):
            mm = nc.tensor.matmul

            def scores(b, k):
                g, j, lo = cols(k)
                n = b * NS + k
                if j == 0:
                    pe.wait_ge(kt_ready, DC * (b * NG + g + 1))
                atleast(pe, ah_ready, n - 1)
                o = ps[:, k % 2, lo:GQ]
                diag = j >= GT * g
                for c in range(DC):
                    last = mm(o, k_t[:, c, j * P:(j + 1) * P], q_t[:, c, g * GQ + lo:(g + 1) * GQ],
                              start=(c == 0), stop=(c == DC - 1 and not diag))
                if diag:
                    last = mm(ps[:, k % 2, lo:lo + P], identb[:, :], maskb[:, :], start=False, stop=True)
                last.then_inc(scores_ready, 1)

            def values(b, k):
                g, j, lo = cols(k)
                n = b * NS + k
                r = k % RING
                if j == 0:
                    atleast(pe, v_ready, b * NG + g + 1)
                    atleast(pe, ot_ready, DC * (b * NG + g - 1))
                pe.wait_ge(ah_ready, n + 1)
                pe.wait_ge(al_ready, n + 1)
                for c in range(DC):
                    o = ps[:, 2 + 2 * (g % 2) + c, lo:GQ]
                    vh = v_hl[:, 0, j, c * P:(c + 1) * P]
                    vl = v_hl[:, 1, j, c * P:(c + 1) * P]
                    end = j == GT * g + GT - 1
                    mm(o, vh, hl_ring[:, 0, r, lo:GQ], start=(j == 0), stop=False)
                    mm(o, vh, hl_ring[:, 1, r, lo:GQ], start=False, stop=False)
                    last = mm(o, vl, hl_ring[:, 0, r, lo:GQ], start=False, stop=end)
                last.then_inc(pv_done, 1)

            def turn_signs(b, q):
                n = b * NG + q
                pe.wait_ge(sgn_ready, n + 1)
                o = ps[:, M1, :].bitcast(BF16).rearrange("p (c t) -> p c t", c=DC)
                for c in range(DC):
                    for i in range(GT):
                        last = nc.tensor.transpose(o[:, c, i * P:(i + 1) * P], sgn[:, i, c * P:(c + 1) * P],
                                                   identb[:, :])
                last.then_inc(sgn_turned, 1)

            def back(G, par):
                pe.wait_ge(ot_ready, DC * (G + 1))
                o = ps[:, M0:M1 + 1, :].rearrange("p a (i d) -> p (a i) d", d=D)
                for i in range(GT):
                    for c in range(DC):
                        last = nc.tensor.transpose(o[:, i, c * P:(c + 1) * P],
                                                   o_t[:, par, c, i * P:(i + 1) * P], ident[:, :])
                last.then_inc(back_done, 1)

            def turn_x1(G, par):
                pe.wait_ge(x1_ready, (G + 1) * GT)
                for i in range(GT):
                    for c in range(DC):
                        last = nc.tensor.transpose(ps[:, M0 + c, i * P:(i + 1) * P],
                                                   xrow[:, par, i, c * P:(c + 1) * P], ident[:, :])
                last.then_inc(x1_turned, 1)

            def router(G):
                pe.wait_ge(x1t_ready, DC * (G + 1))
                for i in range(GT):
                    for c in range(DC):
                        last = mm(ps[:, M0, i * E:(i + 1) * E], x1_t[:, c, i * P:(i + 1) * P], w_r[:, c, :],
                                  start=(c == 0), stop=(c == DC - 1))
                last.then_inc(logits_done, 1)

            def counts(G):
                pe.wait_ge(hot_ready, G + 1)
                pe.wait_ge(seen_ready, G + 1)
                for i in range(GT):
                    o = ps[:, M1, i * E:(i + 1) * E]
                    mm(o, tri[:, :], hot[:, i, :], start=True, stop=False)
                    for h in range(i):
                        mm(o, onesb[:, :], hot[:, h, :], start=False, stop=False)
                    last = mm(o, onesb[:, :], seen[:, :], start=False, stop=True)
                last.then_inc(counts_done, 1)

            def batch(b, first, last):
                for k in range(NS):
                    if k == 0:
                        scores(b, 0)
                        scores(b, 1)
                    if k + 2 < NS:
                        scores(b, k + 2)
                    values(b, k)
                    for g in range(NG):
                        if g == 3 and first:
                            continue
                        G = (b - 1 if g == 3 else b) * NG + g
                        prepared = b * NG + (2 if g == 3 else 3 if g == 0 else 4)
                        if k == TAIL_BACK[g]:
                            atleast(pe, lg_ready, G)
                            atleast(pe, pos_read, G)
                            pe.wait_ge(qt_ready, prepared)
                            back(G, g % 2)
                        if k == TAIL_TURN[g]:
                            pe.wait_ge(res_ready, G + 1)
                            pe.wait_ge(qt_ready, prepared + (1 if g in (3, 0) else 0))
                            turn_x1(G, g % 2)
                        if k == TAIL_ROUTE[g]:
                            router(G)
                        if k == TAIL_COUNT[g]:
                            counts(G)
                    for q in range(NG):
                        if k == PREP[q] and not (q < 2 and last):
                            bb = b + 1 if q < 2 else b
                            tails = b * NG + {2: 0, 3: 1, 0: 3, 1: 3}[q]
                            atleast(pe, res_ready, tails)
                            if q < 2:
                                pe.wait_ge(pos_read, tails)
                            atleast(pe, qt_ready, bb * NG + q)
                            turn_signs(bb, q)

            pe.wait_ge(consts, 8)
            turn_signs(0, 0)
            pe.wait_ge(qt_ready, 1)
            turn_signs(0, 1)
            batch(0, True, False)
            with pe.Fori(1, B - 1) as b:
                batch(b, False, False)
            batch(B - 1, False, True)
            G = B * NG - 1
            pe.wait_ge(lg_ready, G)
            pe.wait_ge(pos_read, G)
            back(G, 1)
            pe.wait_ge(res_ready, G + 1)
            turn_x1(G, 1)
            router(G)
            counts(G)

            def turn_x(R, i):
                e, s = R * SLOT_W + i, i % SLOT_X
                pe.wait_ge(xs_in[s], 32 * (R * (SLOT_W // SLOT_X) + i // SLOT_X + 1))
                atleast(pe, xh_ready, e)
                atleast(pe, xl_ready, e)
                for c in range(DC):
                    for t in range(CT):
                        n = P if t < CFULL else CREST
                        last = nc.tensor.transpose(ps[:, c, t * P:t * P + n], xs[0:n, s, t, c * P:(c + 1) * P],
                                                   ident[0:n, 0:n])
                last.then_inc(xs_turned, 1)

            def gate_up(R, i, f):
                e, p = R * SLOT_W + i, i % 2
                if f == 0:
                    pe.wait_ge(wlgu_ready, e + 1)
                    pe.wait_ge(xh_ready, e + 1)
                    pe.wait_ge(xl_ready, e + 1)
                atleast(pe, hid_step, 4 * e + 2 * f - 2)
                for u in range(2):
                    o = ps[:, 2 + 2 * f + u, 0:CAP]
                    for c in range(DC):
                        wh = w_h[:, p, 2 * u + c, f * P:(f + 1) * P]
                        wl = w_l[:, p, 2 * u + c, f * P:(f + 1) * P]
                        mm(o, wh, x_h[:, p, c, :], start=(c == 0), stop=False)
                        mm(o, wh, x_l[:, p, c, :], start=False, stop=False)
                        last = mm(o, wl, x_h[:, p, c, :], start=False, stop=(c == DC - 1))
                last.then_inc(gu_done, 1)

            def down(R, i):
                e, p = R * SLOT_W + i, i % 2
                pe.wait_ge(hh_ready, FC * (e + 1))
                pe.wait_ge(hl_ready, FC * (e + 1))
                pe.wait_ge(whd_ready, e + 1)
                pe.wait_ge(wld_ready, e + 1)
                for t in range(CT):
                    n = P if t < CFULL else CREST
                    o = ps[0:n, 6 + t // 2, (t % 2) * D:(t % 2 + 1) * D]
                    for f in range(FC):
                        wh, wl = w_h[:, p, 4 + f, :], w_l[:, p, 4 + f, :]
                        hh, hl = h_h[:, p, f, t * P:t * P + n], h_l[:, p, f, t * P:t * P + n]
                        mm(o, hh, wh, start=(f == 0), stop=False)
                        mm(o, hh, wl, start=False, stop=False)
                        last = mm(o, hl, wh, start=False, stop=(f == FC - 1))
                    last.then_inc(y_done, 1)

            def expert(R, i, first=False, last=False):
                gate_up(R, i, 0)
                if not first:
                    down(R, i - 1)
                if not last:
                    turn_x(R, i + 1)
                gate_up(R, i, 1)

            pe.wait_ge(lg_ready, B * NG)
            pe.wait_ge(pos_read, B * NG)
            turn_x(0, 0)
            expert(0, 0, first=True)
            with pe.Fori(0, (E - 2) // SLOT_W) as R:
                for i in range(1, SLOT_W + 1):
                    expert(R, i)
            RL = (E - 2) // SLOT_W
            expert(RL, 1, last=True)
            down(RL, 1)

        @block.vector
        def _(dve):
            v_ = nc.vector
            dve.wait_ge(bsgn_ready, 1)
            v_.tensor_tensor(qk_sgn[:, :], bsgn[:, 0, :], bsgn[:, 1, :], ALU.mult).then_inc(qksgn_ready, 1)
            v_.memset(seen[:, :], 0.0).then_inc(seen_ready, 1)
            dve.wait_ge(qksgn_ready, 1)
            dve.wait_ge(consts, 8)

            def queries_keys(b, q):
                n = b * NG + q
                dve.wait_ge(sgn_turned, n + 1)
                o = ps[:, M1, :].bitcast(BF16).rearrange("p (c t) -> p c t", c=DC)
                sl = slice(q * GQ, (q + 1) * GQ)
                v_.tensor_copy(q_t[:, :, sl], o).then_inc(qt_ready, 1)
                dve.wait_ge(qt_ready, n + 1)
                for c in range(DC):
                    v_.tensor_scalar(k_t[:, c, sl], q_t[:, c, sl], qk_sgn[:, c:c + 1], None, ALU.mult)\
                        .then_inc(kt_ready, 1)

            def low(b, k):
                g, j, lo = cols(k)
                n = b * NS + k
                r = k % RING
                dve.wait_ge(a_ready, n + 1)
                dve.wait_ge(ah_ready, n + 1)
                atleast(dve, pv_done, n - RING + 1)
                v_.tensor_tensor(hl_ring[:, 1, r, lo:GQ], a_ring[:, r, lo:GQ],
                                 hl_ring[:, 0, r, lo:GQ].bitcast(F32), ALU.subtract).then_inc(al_ready, 1)

            def residual(G):
                dve.wait_ge(back_done, G + 1)
                atleast(dve, x1_ready, G * GT)
                v_.tensor_tensor(res[:, :, :], ps[:, M0:M1 + 1, :].rearrange("p a (i d) -> p (a i) d", d=D),
                                 xall[:, bass.ds(G * GT, GT), :], ALU.add).then_inc(res_ready, 1)
                dve.wait_ge(res_ready, G + 1)
                for i in range(GT):
                    v_.bn_stats(stats[:, i, :], res[:, i, :]).then_inc(stats_step, 1)
                dve.wait_ge(stats_step, (G + 1) * GT)
                atleast(dve, rstd_step, G * 6, settle=True)
                for i in range(GT):
                    v_.bn_aggr(mv[:, i, :], stats[:, i, :]).then_inc(mv_ready, 1)

            def normalise(G, turn, par):
                dve.wait_ge(rstd_step, G * 6 + 2)
                dve.wait_ge(mv_ready, (G + 1) * GT)
                atleast(dve, scattered[par], turn * 16 * GT)
                for i in range(GT):
                    v_.tensor_scalar(xrow[:, par, i, 0:D], res[:, i, :], mv[:, i, 0:1], small[:, 1, i:i + 1],
                                     ALU.subtract, ALU.mult).then_inc(x1_ready, 1)

            SN = 13

            def route(G):
                dve.wait_ge(logits_done, G + 1)
                v_.tensor_copy(lg[:, :, :], ps[:, M0, 0:GT * E].rearrange("p (i e) -> p i e", e=E))\
                    .then_inc(lg_ready, 1)
                atleast(dve, lg_ready, G + 1, settle=True)
                base = G * SN
                for i in range(GT):
                    v_.max(top[:, i, :], lg[:, i, :]).then_inc(route_step, 1)
                atleast(dve, route_step, base + 4, settle=True)
                for i in range(GT):
                    v_.max_index(topi[:, i, :], top[:, i, :], lg[:, i, :]).then_inc(route_step, 1)
                atleast(dve, sg_ready, 2 * G)
                v_.tensor_tensor(below[:, :, :], lg[:, :, :], top[:, :, 0:1].broadcast_to([P, GT, E]),
                                 ALU.subtract).then_inc(below_ready, 1)
                dve.wait_ge(route_step, base + 8)
                v_.tensor_copy(topf[:, :], topi[:, :, 0]).then_inc(route_step, 1)
                dve.wait_ge(route_step, base + 9)
                v_.tensor_tensor(hot[:, :, :], iota_e[:, :, :],
                                 topf[:, :].unsqueeze(2).broadcast_to([P, GT, E]), ALU.is_equal)\
                    .then_inc(hot_ready, 1)

            def place(G, par):
                base = G * SN + 9
                dve.wait_ge(counts_done, G + 1)
                v_.tensor_tensor(pm[:, :, :], hot[:, :, :],
                                 ps[:, M1, 0:GT * E].rearrange("p (i e) -> p i e", e=E), ALU.mult)\
                    .then_inc(pos_read, 1)
                v_.tensor_reduce(hots[:, :], hot[:, :, :].rearrange("p i e -> p e i"), AX_X, ALU.add)\
                    .then_inc(route_step, 1)
                dve.wait_ge(pos_read, G + 1)
                v_.tensor_reduce(rt[:, 0, :], pm[:, :, :], AX_X, ALU.add).then_inc(route_step, 1)
                dve.wait_ge(route_step, base + 1)
                v_.tensor_tensor(seen[:, :], seen[:, :], hots[:, :], ALU.add).then_inc(seen_ready, 1)
                dve.wait_ge(route_step, base + 2)
                v_.tensor_scalar(rt[:, 1, :], rt[:, 0, :], CAP + 0.5, SKIP, ALU.is_gt, ALU.mult)\
                    .then_inc(route_step, 1)
                v_.scalar_tensor_tensor(out=rt[:, 2, :], in0=topf[:, :], scalar=float(CAP), in1=rt[:, 0, :],
                                        op0=ALU.mult, op1=ALU.add).then_inc(route_step, 1)
                dve.wait_ge(route_step, base + 4)
                v_.scalar_tensor_tensor(out=slot[:, par, :], in0=rt[:, 2, :], scalar=-1.0, in1=rt[:, 1, :],
                                        op0=ALU.add, op1=ALU.add).then_inc(slot_ready, 1)
                dve.wait_ge(sg_ready, 2 * G + 2)
                v_.reciprocal(rneg[:, :, :], sg[:, 1, :, :]).then_inc(gate_step, 1)
                dve.wait_ge(gate_step, 3 * G + 1)
                v_.scalar_tensor_tensor(out=pm[:, :, :], in0=sg[:, 0, :, :], scalar=2.0, in1=rneg[:, :, :],
                                        op0=ALU.mult, op1=ALU.mult).then_inc(gate_step, 1)
                dve.wait_ge(gate_step, 3 * G + 2)
                v_.tensor_reduce(rt[:, 3, :], pm[:, :, :], AX_X, ALU.add).then_inc(gate_step, 1)
                dve.wait_ge(gate_step, 3 * G + 3)
                v_.reciprocal(xrow[:, par, :, D], rt[:, 3, :]).then_inc(gate_ready, 1)

            def batch(b, first, last):
                for k in range(NS + 1):
                    if k < NS:
                        low(b, k)
                    for g in range(NG):
                        if g == 3 and first:
                            continue
                        G = (b - 1 if g == 3 else b) * NG + g
                        turn = 2 * b + {3: -1, 0: 0, 1: 0, 2: 1}[g]
                        if k == TAIL_BACK[g] + 1:
                            residual(G)
                        if k == TAIL_BACK[g] + 2:
                            normalise(G, turn, g % 2)
                        if k == TAIL_ROUTE[g] + 1:
                            route(G)
                        if k == TAIL_COUNT[g] + 1:
                            place(G, g % 2)
                    for q in range(NG):
                        if k == PREP[q] + 1 and not (q < 2 and last):
                            queries_keys(b + 1 if q < 2 else b, q)

            queries_keys(0, 0)
            queries_keys(0, 1)
            batch(0, True, False)
            with dve.Fori(1, B - 1) as b:
                batch(b, False, False)
            batch(B - 1, False, True)
            G = B * NG - 1
            residual(G)
            normalise(G, 2 * B - 1, 1)
            route(G)
            place(G, 1)

            v_.memset(zmv[:, :, :, :], 0.0).then_inc(zmv_clear, 1)
            dve.wait_ge(zmv_clear, 1)
            dve.wait_ge(pv_done, B * NS)

            def low_d(R, i):
                e, s, p = R * SLOT_W + i, i % SLOT_W, i % 2
                dve.wait_ge(whd_ready, e + 1)
                atleast(dve, y_done, (e - 1) * CT)
                v_.tensor_tensor(w_l[:, p, 4:6, :], raw[:, s, 4:6, :], w_h[:, p, 4:6, :].bitcast(F32),
                                 ALU.subtract).then_inc(wld_ready, 1)

            def low_x(R, i):
                e, p = R * SLOT_W + i, i % 2
                dve.wait_ge(xh_ready, e + 1)
                atleast(dve, gu_done, 2 * (e - 1))
                v_.tensor_tensor(x_l[:, p, :, :], ps[:, 0:DC, 0:CAP], x_h[:, p, :, :].bitcast(F32),
                                 ALU.subtract).then_inc(xl_ready, 1)

            def hidden(R, i, f):
                e, p = R * SLOT_W + i, i % 2
                dve.wait_ge(sig_ready, FC * e + f + 1)
                v_.tensor_tensor(act_t[:, f, :], act_s[:, f, :], ps[:, 2 + 2 * f, 0:CAP], ALU.mult)\
                    .then_inc(hid_step, 1)
                dve.wait_ge(hid_step, 4 * e + 2 * f + 1)
                atleast(dve, hh_ready, FC * e + f - 1)
                v_.tensor_tensor(act_h[:, f, :], act_t[:, f, :], ps[:, 3 + 2 * f, 0:CAP], ALU.mult)\
                    .then_inc(hid_step, 1)

            def low_hidden(R, i, f):
                e, p = R * SLOT_W + i, i % 2
                dve.wait_ge(hh_ready, FC * e + f + 1)
                atleast(dve, y_done, (e - 1) * CT)
                v_.tensor_tensor(h_l[:, p, f, :], act_h[:, f, :], h_h[:, p, f, :].bitcast(F32),
                                 ALU.subtract).then_inc(hl_ready, 1)

            def combine(R, i):
                e, s, p = R * SLOT_W + i, i % SLOT_X, i % 2
                atleast(dve, os_ready, e * CT)
                for t in range(CT):
                    n = P if t < CFULL else CREST
                    dve.wait_ge(y_done, e * CT + min(CT, t // 2 * 2 + 2))
                    dve.wait_ge(xs_in[s], 32 * (R * (SLOT_W // SLOT_X) + i // SLOT_X + 1))
                    v_.scalar_tensor_tensor(out=z[0:n, t, :], in0=ps[0:n, 6 + t // 2, (t % 2) * D:(t % 2 + 1) * D],
                                            scalar=xs[0:n, s, t, D:D + 1], in1=xs[0:n, s, t, 0:D],
                                            op0=ALU.mult, op1=ALU.add).then_inc(z_step, 1)
                for t in range(CT):
                    n = P if t < CFULL else CREST
                    dve.wait_ge(z_step, e * CT + t + 1)
                    v_.bn_stats(zst[0:n, t, :], z[0:n, t, :]).then_inc(zst_step, 1)
                for t in range(CT):
                    n = P if t < CFULL else CREST
                    atleast(dve, zst_step, e * CT + t + 1, settle=True)
                    v_.bn_aggr(zmv[0:n, p, t, :], zst[0:n, t, :]).then_inc(zmv_ready, 1)

            def second_norm(R, i):
                e, p = R * SLOT_W + i, i % 2
                dve.wait_ge(zrs_ready, e + 1)
                dve.wait_ge(zmv_ready, (e + 1) * CT)
                atleast(dve, os_out[p], 16 * CT * (R * (SLOT_W // 2) + i // 2))
                for t in range(CT):
                    n = P if t < CFULL else CREST
                    v_.tensor_scalar(o_s[0:n, p, t, :], z[0:n, t, :], zmv[0:n, p, t, 0:1], zrs[0:n, p, 1, t:t + 1],
                                     ALU.subtract, ALU.mult).then_inc(os_ready, 1)

            def expert(R, i, first=False, last=False):
                hidden(R, i, 0)
                low_hidden(R, i, 0)
                if not first:
                    combine(R, i - 1)
                if not last:
                    low_x(R, i + 1)
                    low_d(R, i + 1)
                if not first:
                    second_norm(R, i - 1)
                hidden(R, i, 1)
                low_hidden(R, i, 1)

            low_d(0, 0)
            low_x(0, 0)
            expert(0, 0, first=True)
            with dve.Fori(0, (E - 2) // SLOT_W) as R:
                for i in range(1, SLOT_W + 1):
                    expert(R, i)
            RL = (E - 2) // SLOT_W
            expert(RL, 1, last=True)
            combine(RL, 1)
            second_norm(RL, 1)


_INS = ["L0_attn_x", "L0_attn_bv_q", "L0_attn_bv_k", "L0_attn_bv_v", "L0_ffn_w_router", "L0_ffn_w_gate",
        "L0_ffn_w_up", "L0_ffn_w_down"]
_OUTS = [((4, 2048, 256), "float32")]


def kernel(**inputs):
    import numpy as _np
    import concourse.bacc as _bacc
    from concourse import mybir as _mybir
    from concourse.bass_utils import run_bass_kernel_spmd as _run

    nc = _bacc.Bacc("TRN2", target_bir_lowering=False, num_devices=1)
    arrays, args = {}, []
    for name in _INS:
        a = _np.ascontiguousarray(inputs[name])
        arrays[f"in_{name}_dram"] = a
        args.append(nc.dram_tensor(f"in_{name}_dram", a.shape, _mybir.dt.from_np(a.dtype), kind="ExternalInput").ap())
    for i, (shape, dtype) in enumerate(_OUTS):
        dt = _mybir.dt.from_np(_np.dtype(dtype))
        args.append(nc.dram_tensor(f"out_{i}_dram", shape, dt, kind="ExternalOutput").ap())
    bass_postln_attn_moe_kernel(nc, *args)
    r = _run(nc, [arrays], core_ids=[0])
    got = tuple(r.results[0][f"out_{i}_dram"] for i in range(len(_OUTS)))
    return got[0]
```

```python
from contextlib import ExitStack

import numpy as np

import concourse.bass as bass
from concourse import mybir

ALU = mybir.AluOpType
ACT = mybir.ActivationFunctionType
AX_X = mybir.AxisListType.X
F32 = mybir.dt.float32
F32R = mybir.dt.float32r
BF16 = mybir.dt.bfloat16
U32 = mybir.dt.uint32

P = 128
EPS = 1e-5
MASKED = -30000.0
SKIP = 65536.0
NOBODY = 1 << 20

GT = 4
GQ = GT * P
RING = 4

SCALE = {3: 1, 0: 5, 1: 14, 2: 26}
BACK = {3: 2, 0: 6, 1: 20, 2: 30}
SUM = {3: 3, 0: 7, 1: 21, 2: 31}
STATS = {3: 4, 0: 8, 1: 22, 2: 32}
NORM = {3: 7, 0: 11, 1: 25, 2: 35}
TURN = {3: 8, 0: 15, 1: 25, 2: 35}
COPY = {3: 10, 0: 17, 1: 27, 2: 37}
ROUTE = {3: 10, 0: 17, 1: 27, 2: 37}
PICK = {3: 11, 0: 18, 1: 28, 2: 38}
COUNT = {3: 12, 0: 19, 1: 29, 2: 39}
PLACE = {3: 13, 0: 20, 1: 30, 2: 40}
GATE = {3: 14, 0: 21, 1: 31, 2: 40}
PREP = {2: 4, 3: 13, 0: 31, 1: 33}
QK = {q: k + 1 for q, k in PREP.items()}
VHIGH = {q: k + 1 for q, k in PREP.items()}


def bass_postln_attn_moe_kernel(nc, x, bv_q, bv_k, bv_v, w_router, w_gate, w_up, w_down, out):
    B, T, D = x.shape
    E, _, F = w_gate.shape
    NT = B * T // P
    NG = T // GQ
    DC, FC = D // P, F // P
    N_TOK = B * T
    CAP = -(-5 * N_TOK // (4 * E))
    ROW = D + 2
    CT = -(-CAP // P)
    CFULL = CAP // P
    CREST = CAP - CFULL * P
    SLOTS = E * CAP
    ZR = 2
    assert NG == 4 and DC == 2 and FC == 2 and NT == 64 and CREST > 0 and E == 32
    STEPS = [(g, j) for g in range(NG) for j in range(GT * g + GT)]
    OFF = [0, 4, 12, 24]
    NS = len(STEPS)
    END = [OFF[g] + GT * g + GT for g in range(NG)]
    U = 4
    assert (E - 4) % U == 0

    x_rows = x.rearrange("b t d -> (b t) d")
    out_rows = out.rearrange("b t d -> (b t) d")
    buf = nc.dram_tensor("expert_rows", [SLOTS, ROW], F32)
    buf_rows = buf.ap()

    with ExitStack() as ctx:
        def sb(name, shape, dt):
            return ctx.enter_context(nc.sbuf_tensor(name, shape, dt))

        def sem(name):
            return ctx.enter_context(nc.semaphore(name))

        ps = ctx.enter_context(nc.psum_tensor("ps", [P, 8, 512], F32))
        ident = sb("ident", [P, P], F32)
        identb = sb("identb", [P, P], BF16)
        tri = sb("tri", [P, P], BF16)
        onesb = sb("onesb", [P, P], BF16)
        maskb = sb("maskb", [P, P], BF16)
        iota_e = sb("iota_e", [P, GT, E], F32)
        tok = sb("tok", [P, GT], U32)
        mhalf = sb("mhalf", [P, GT], F32)
        mone = sb("mone", [P, GT], F32)
        bvec = sb("bvec", [P, 3, DC], F32)
        bsgn = sb("bsgn", [P, 3, DC], F32)
        qk_sgn = sb("qk_sgn", [P, DC], F32)
        w_r = sb("w_r", [P, DC, E], F32)

        xall = sb("xall", [P, NT, D], F32)
        v_hl = sb("v_hl", [P, 2, T // P, D], F32R)
        sgn = sb("sgn", [P, GT, D], BF16)
        q_t = sb("q_t", [P, DC, T], BF16)
        k_t = sb("k_t", [P, DC, T], BF16)
        a_ring = sb("a_ring", [P, RING, GQ], F32)
        hl_ring = sb("hl_ring", [P, 2, RING, GQ], F32R)
        o_t = sb("o_t", [P, 2, DC, GQ], F32)
        res = sb("res", [P, GT, D], F32)
        stats = sb("stats", [P, GT, 6], F32)
        mv = sb("mv", [P, GT, 2], F32)
        small = sb("small", [P, 8, GT], F32)
        xrow = sb("xrow", [P, 2, GT, ROW], F32)
        alone = sb("alone", [P, 2, GT, D], F32)
        x1_t = sb("x1_t", [P, DC, GQ], F32)
        lg = sb("lg", [P, GT, E], F32)
        top = sb("top", [P, GT, 8], F32)
        topi = sb("topi", [P, GT, 8], U32)
        topf = sb("topf", [P, GT], F32)
        hot = sb("hot", [P, GT, E], BF16)
        below = sb("below", [P, GT, E], F32)
        sg = sb("sg", [P, 2, GT, E], F32)
        quot = sb("quot", [P, GT, E], F32)
        pm = sb("pm", [P, GT, E], F32)
        hots = sb("hots", [P, E], F32)
        seen = sb("seen", [P, E], BF16)
        rt = sb("rt", [P, 6, GT], F32)
        slot = sb("slot", [P, 2, GT], U32)

        raw = xall[:, 0:6 * U, :].rearrange("p (s k) f -> p s k f", k=6)
        w_h, w_l = (v_hl[:, n, 0:4 * 2, :].rearrange("p (s k) f -> p s k f", s=2) for n in range(2))
        r_flat = hl_ring[:, :, :, :].rearrange("p a r t -> p (a r t)")
        XN = DC * CAP
        x_h, x_l = (r_flat[:, n * 2 * XN:(n + 1) * 2 * XN].rearrange("p (s k t) -> p s k t", s=2, t=CAP)
                    for n in range(2))
        a_flat = a_ring[:, :, :].rearrange("p r t -> p (r t)")
        HN = FC * CAP
        act_s = a_flat[:, 0:HN].rearrange("p (k t) -> p k t", k=FC)
        act_h = a_flat[:, HN:3 * HN].rearrange("p (s k t) -> p s k t", s=2, t=CAP)
        xs = sb("xs", [P, U, CT, ROW], F32)
        zero = xs[:, 0, :, :].rearrange("p a w -> p (a w)")[:, 0:ZR * ROW]
        z = o_t[:, :, :, :].rearrange("p a c t -> p a (c t)")[:, :, 0:CT * D].rearrange("p a (t d) -> p a t d", d=D)
        zst = sb("zst", [P, CT, 6], F32)
        zmv = sb("zmv", [P, 2, CT, 2], F32)
        zrs = sb("zrs", [P, 2, 4, CT], F32)
        ids = sb("ids", [P, U, CT], U32)
        o_s = alone[:, :, 0:CT, :]

        x_in = [sem(f"x_in{q}") for q in range(NG)]
        small_in = sem("small_in")
        zero_step = sem("zero_step")
        zero_out = sem("zero_out")
        consts = sem("consts")
        consts_step = sem("consts_step")
        bsgn_ready = sem("bsgn_ready")
        qksgn_ready = sem("qksgn_ready")
        sgn_ready = sem("sgn_ready")
        vh_ready = sem("vh_ready")
        v_ready = sem("v_ready")
        sgn_turned = sem("sgn_turned")
        qt_ready = sem("qt_ready")
        kt_ready = sem("kt_ready")
        scores_ready = sem("scores_ready")
        a_ready = sem("a_ready")
        ah_ready = sem("ah_ready")
        al_ready = sem("al_ready")
        pv_done = sem("pv_done")
        ot_ready = sem("ot_ready")
        back_done = sem("back_done")
        res_ready = sem("res_ready")
        stats_step = sem("stats_step")
        mv_ready = sem("mv_ready")
        rstd_step = sem("rstd_step")
        x1_ready = sem("x1_ready")
        x1_turned = sem("x1_turned")
        x1t_ready = sem("x1t_ready")
        logits_done = sem("logits_done")
        lg_ready = sem("lg_ready")
        route_step = sem("route_step")
        hot_ready = sem("hot_ready")
        below_ready = sem("below_ready")
        sg_ready = sem("sg_ready")
        counts_done = sem("counts_done")
        pos_read = sem("pos_read")
        seen_ready = sem("seen_ready")
        gate_step = sem("gate_step")
        gate_ready = sem("gate_ready")
        slot_ready = sem("slot_ready")
        tok_step = sem("tok_step")
        alone_ready = sem("alone_ready")
        alone_out = [sem(f"alone_out{i}") for i in range(2)]
        scattered = [sem(f"scattered{i}") for i in range(2)]

        raw_in = [sem(f"raw_in{i}") for i in range(U)]
        xs_in = [sem(f"xs_in{i}") for i in range(U)]
        xs_turned = sem("xs_turned")
        xh_ready = sem("xh_ready")
        xl_ready = sem("xl_ready")
        wh_ready = sem("wh_ready")
        wl_ready = sem("wl_ready")
        silu_ready = sem("silu_ready")
        h_ready = sem("h_ready")
        gu_done = sem("gu_done")
        y_done = sem("y_done")
        z_step = sem("z_step")
        zst_step = sem("zst_step")
        zmv_clear = sem("zmv_clear")
        zmv_ready = sem("zmv_ready")
        zr_step = sem("zr_step")
        zrs_ready = sem("zrs_ready")
        ids_half = sem("ids_half")
        ids_ready = sem("ids_ready")
        os_ready = sem("os_ready")
        os_out = [sem(f"os_out{i}") for i in range(2)]

        def atleast(eng, s, value, settle=False):
            if isinstance(value, int) and value <= 0:
                return
            if settle and not isinstance(value, int):
                value = eng.to_reg(value)
                eng.wait_ge(consts, 9)
            eng.wait_ge(s, value)

        block = ctx.enter_context(nc.Block())
        M0, M1 = 6, 7

        def cols(k):
            g, j = STEPS[k]
            return g, j, max(0, j - GT * g) * P

        @block.sync
        def _(sp):
            def load_x(b, q):
                src = x[b, q * GQ:(q + 1) * GQ, :].rearrange("(i p) d -> p i d", p=P)
                sp.dma_start(xall[:, bass.ds(b * (T // P) + GT * q, GT), :], src).then_inc(x_in[q], 16)

            load_x(0, 0)
            for n, v in enumerate((bv_q, bv_k, bv_v)):
                sp.dma_start(bvec[:, n, :], v.rearrange("(c p) -> p c", p=P),
                             allow_slow_non_contiguous=True).then_inc(small_in, 16)
            sp.dma_start(w_r[:, :, :], w_router.rearrange("(c p) e -> p c e", p=P)).then_inc(small_in, 16)
            for q in range(1, NG):
                load_x(0, q)
            sp.wait_ge(zero_step, 3)
            zrows = buf_rows.rearrange("(n p r) w -> n p (r w)", p=P, r=ZR)
            for n in range(SLOTS // (P * ZR)):
                sp.dma_start(zrows[n], zero).then_inc(zero_out, 16)

            def store_alone(G, par):
                atleast(sp, alone_ready, G + 1)
                dst = out_rows[bass.ds(G * GQ, GQ), :].rearrange("(i p) d -> p i d", p=P)
                sp.dma_start(dst, alone[:, par, :, :]).then_inc(alone_out[par], 16)

            with sp.Fori(1, B) as b:
                for q in range(NG):
                    sp.wait_ge(v_ready, (b - 1) * NG + q + 1)
                    sp.wait_ge(sgn_ready, (b - 1) * NG + q + 1)
                    load_x(b, q)
                    store_alone((b - 1) * NG + q, q % 2)

            def load_raw(e, s):
                for n, w in enumerate((w_gate, w_up, w_down)):
                    sp.dma_start(raw[:, s, 2 * n:2 * n + 2, :],
                                 w[e].rearrange("(c p) f -> p c f", p=P)).then_inc(raw_in[s], 16)

            def load_xs(e, s):
                rows = buf_rows[bass.ds(e * CAP, CAP), :]
                sp.dma_start(xs[:, s, 0:CFULL, :],
                             rows[0:CFULL * P, :].rearrange("(i p) w -> p i w", p=P)).then_inc(xs_in[s], 16)
                sp.dma_start(xs[0:CREST, s, CFULL, :], rows[CFULL * P:CAP, :]).then_inc(xs_in[s], 16)

            last = (B - 1) * NG
            for s in range(U):
                sp.wait_ge(res_ready, (6 * s + 5) // GT + 1)
                load_raw(s, s)
            for q in range(NG):
                store_alone(last + q, q % 2)
            for par in range(2):
                sp.wait_ge(scattered[par], 16 * GT * B * NG // 2)
            for e in range(U):
                load_xs(e, e)

            with sp.Fori(0, (E - U) // U) as R:
                for i in range(U):
                    e = R * U + i
                    sp.wait_ge(z_step, (e + 1) * CT)
                    sp.wait_ge(ids_ready, e + 1)
                    load_xs(e + U, i)
                    sp.wait_ge(wh_ready, e + 1)
                    sp.wait_ge(wl_ready, e + 1)
                    sp.wait_ge(y_done, (e + 1) * CT)
                    load_raw(e + U, i)
            for par in range(2):
                sp.wait_ge(alone_out[par], 16 * B * NG // 2)

        @block.gpsimd
        def _(pool):
            g_ = nc.gpsimd
            g_.memset(zero, 0.0).then_inc(zero_step, 1)
            pool.wait_ge(zero_step, 1)
            g_.memset(zero.rearrange("p (r w) -> p r w", w=ROW)[:, :, D + 1].bitcast(U32), NOBODY)\
                .then_inc(zero_step, 2)
            g_.memset(ident[:, :], 0.0).then_inc(consts_step, 1)
            g_.memset(identb[:, :], 0.0).then_inc(consts_step, 1)
            g_.memset(tri[:, :], 1.0).then_inc(consts_step, 1)
            g_.memset(maskb[:, :], 0.0).then_inc(consts_step, 1)
            g_.memset(onesb[:, :], 1.0).then_inc(consts, 1)
            g_.memset(mhalf[:, :], -0.5).then_inc(consts, 1)
            g_.memset(mone[:, :], -1.0).then_inc(consts, 1)
            pool.wait_ge(consts_step, 4)
            for m in (ident, identb):
                g_.affine_select(out=m[:, :], in_=m[:, :], compare_op=ALU.not_equal, fill=1.0, base=0,
                                 pattern=[[-1, P]], channel_multiplier=1).then_inc(consts, 1)
            g_.affine_select(out=tri[:, :], in_=tri[:, :], compare_op=ALU.is_ge, fill=0.0, base=0,
                             pattern=[[1, P]], channel_multiplier=-1).then_inc(consts, 1)
            g_.affine_select(out=maskb[:, :], in_=maskb[:, :], compare_op=ALU.is_ge, fill=MASKED, base=0,
                             pattern=[[1, P]], channel_multiplier=-1).then_inc(consts, 1)
            g_.iota(iota_e[:, :, :], pattern=[[0, GT], [1, E]], base=0, channel_multiplier=0,
                    allow_small_or_imprecise_dtypes=True).then_inc(consts, 1)
            g_.iota(tok[:, :], pattern=[[P, GT]], base=0, channel_multiplier=1,
                    allow_small_or_imprecise_dtypes=True).then_inc(consts, 1)

            def values_low(b, q):
                sl = slice(GT * q, GT * q + GT)
                atleast(pool, vh_ready, b * NG + q + 1, settle=True)
                g_.tensor_tensor(v_hl[:, 1, sl, :], xall[:, bass.ds(b * (T // P) + GT * q, GT), :],
                                 v_hl[:, 0, sl, :].bitcast(F32), ALU.subtract).then_inc(v_ready, 1)

            RN = 6

            def rstd(G, par):
                atleast(pool, mv_ready, (G + 1) * GT, settle=True)
                atleast(pool, alone_ready, G, settle=True)
                base = G * RN
                atleast(pool, x1_ready, G * GT, settle=True)
                var = mv[:, :, 1]
                g_.tensor_scalar(small[:, 0, :], var, EPS, None, ALU.add).then_inc(rstd_step, 1)
                atleast(pool, rstd_step, base + 1, settle=True)
                g_.tensor_tensor(small[:, 1, :], small[:, 0, :], mhalf[:, :], ALU.pow).then_inc(rstd_step, 1)
                atleast(pool, rstd_step, base + 2, settle=True)
                g_.tensor_tensor(small[:, 2, :], var, small[:, 1, :], ALU.mult).then_inc(rstd_step, 1)
                atleast(pool, rstd_step, base + 3, settle=True)
                g_.tensor_tensor(small[:, 3, :], small[:, 2, :], small[:, 1, :], ALU.mult).then_inc(rstd_step, 1)
                atleast(pool, rstd_step, base + 4, settle=True)
                g_.tensor_scalar(small[:, 4, :], small[:, 3, :], EPS / 4, None, ALU.add).then_inc(rstd_step, 1)
                atleast(pool, rstd_step, base + 5, settle=True)
                g_.tensor_tensor(small[:, 5, :], small[:, 4, :], mhalf[:, :], ALU.pow).then_inc(rstd_step, 1)

            def rows_alone(G, half, par):
                atleast(pool, rstd_step, G * RN + RN, settle=True)
                atleast(pool, x1_ready, (G + 1) * GT, settle=True)
                atleast(pool, alone_out[par], half * 16, settle=True)
                g_.tensor_tensor(alone[:, par, :, :], xrow[:, par, :, 0:D],
                                 small[:, 5, :].unsqueeze(2).broadcast_to([P, GT, D]), ALU.mult)\
                    .then_inc(alone_ready, 1)
                g_.tensor_copy(xrow[:, par, :, D + 1].bitcast(U32), tok[:, :]).then_inc(tok_step, 1)
                atleast(pool, tok_step, G * 2 + 1, settle=True)
                g_.tensor_scalar(tok[:, :], tok[:, :], float(GQ), None, ALU.add).then_inc(tok_step, 1)
                atleast(pool, tok_step, G * 2 + 2, settle=True)

            def scatter(G, par):
                atleast(pool, gate_ready, G + 1, settle=True)
                atleast(pool, slot_ready, G + 1, settle=True)
                for i in range(GT):
                    g_.indirect_dma_start(
                        out=buf_rows, out_offset=bass.IndirectOffsetOnAxis(ap=slot[:, par, i:i + 1], axis=0),
                        in_=xrow[:, par, i, :], in_offset=None, bounds_check=SLOTS - 1,
                        oob_is_err=False).then_inc(scattered[par], 16)

            def batch(b, first, last):
                n = b * NG
                if not first:
                    scatter(n - 2, 0)
                    rstd(n - 1, 1)
                values_low(b, 2)
                if not first:
                    rows_alone(n - 1, 2 * b - 1, 1)
                rstd(n, 0)
                if not first:
                    scatter(n - 1, 1)
                rows_alone(n, 2 * b, 0)
                values_low(b, 3)
                if first:
                    pool.wait_ge(zero_out, 16 * (SLOTS // (P * ZR)))
                scatter(n, 0)
                rstd(n + 1, 1)
                rows_alone(n + 1, 2 * b, 1)
                scatter(n + 1, 1)
                rstd(n + 2, 0)
                if not last:
                    values_low(b + 1, 0)
                rows_alone(n + 2, 2 * b + 1, 0)
                if not last:
                    values_low(b + 1, 1)

            values_low(0, 0)
            values_low(0, 1)
            pool.wait_ge(consts, 9)
            batch(0, True, False)
            with pool.Fori(1, B - 1) as b:
                batch(b, False, False)
            batch(B - 1, False, True)
            last = (B - 1) * NG
            scatter(last + 2, 0)

            def numbers(R, n):
                e, p = R * U + n, n % 2
                atleast(pool, xs_in[n % U], 32 * (R + n // U + 1), settle=True)
                if n // 2 > 1 or not isinstance(R, int) or R > 0:
                    atleast(pool, os_out[p], 16 * CT * (R * (U // 2) + n // 2 - 1), settle=True)
                for t, rows in ((slice(0, CFULL), P), (slice(CFULL, CT), CREST)):
                    g_.tensor_copy(ids[0:rows, n % U, t], xs[0:rows, n % U, t, D + 1].bitcast(U32))\
                        .then_inc(ids_half, 1)
                atleast(pool, ids_half, 2 * e + 2, settle=True)
                pool.sem_inc(ids_ready, 1)

            def second_rstd(R, n):
                e, p = R * U + n, n % 2
                atleast(pool, zmv_ready, (e + 1) * CT, settle=True)
                g_.tensor_scalar(zrs[:, p, 0, :], zmv[:, p, :, 1], EPS / 4, None, ALU.add).then_inc(zr_step, 1)
                g_.tensor_tensor(zrs[:, p, 3, :], zmv[:, p, :, 0], mone[:, 0:CT], ALU.mult).then_inc(zr_step, 1)
                atleast(pool, zr_step, 3 * e + 2, settle=True)
                g_.tensor_tensor(zrs[:, p, 1, :], zrs[:, p, 0, :], mhalf[:, 0:CT], ALU.pow)\
                    .then_inc(zr_step, 1)
                atleast(pool, zr_step, 3 * e + 3, settle=True)
                g_.tensor_tensor(zrs[:, p, 2, :], zrs[:, p, 3, :], zrs[:, p, 1, :], ALU.mult)\
                    .then_inc(zrs_ready, 1)

            def store(R, n):
                e, p = R * U + n, n % 2
                atleast(pool, ids_ready, e + 1, settle=True)
                atleast(pool, os_ready, (e + 1) * CT, settle=True)
                for t in range(CT):
                    rows = P if t < CFULL else CREST
                    g_.indirect_dma_start(
                        out=out_rows, out_offset=bass.IndirectOffsetOnAxis(ap=ids[0:rows, n % U, t:t + 1], axis=0),
                        in_=o_s[0:rows, p, t, :], in_offset=None, bounds_check=N_TOK - 1,
                        oob_is_err=False).then_inc(os_out[p], 16)

            rstd(last + 3, 1)
            rows_alone(last + 3, 2 * B - 1, 1)
            scatter(last + 3, 1)
            for par in range(2):
                pool.wait_ge(alone_out[par], 16 * B * NG // 2)

            def turn(R, n):
                if n >= 2:
                    second_rstd(R, n - 2)
                numbers(R, n)
                if n >= 3:
                    store(R, n - 3)

            turn(0, 0)
            turn(0, 1)
            turn(0, 2)
            with pool.Fori(0, (E - 4) // U) as R:
                for n in range(3, 3 + U):
                    turn(R, n)
            RL = (E - 4) // U
            turn(RL, 3)
            second_rstd(RL, 2)
            store(RL, 1)
            second_rstd(RL, 3)
            store(RL, 2)
            store(RL, 3)
            for par in range(2):
                pool.wait_ge(os_out[par], 16 * CT * E // 2)

        @block.scalar
        def _(act):
            s_ = nc.scalar
            act.wait_ge(small_in, 64)
            s_.activation(bsgn[:, :, :], bvec[:, :, :], ACT.Sign).then_inc(bsgn_ready, 1)
            act.wait_ge(bsgn_ready, 1)

            def signs(b, q):
                act.wait_ge(x_in[q], (b + 1) * 16)
                atleast(act, sgn_turned, b * NG + q)
                s_.activation(sgn[:, :, :], xall[:, bass.ds(b * (T // P) + GT * q, GT), :], ACT.Sign)\
                    .then_inc(sgn_ready, 1)

            def values_high(b, q):
                atleast(act, x_in[q], (b + 1) * 16, settle=True)
                atleast(act, pv_done, (b - 1) * NS + OFF[3] + GT * q + GT)
                atleast(act, v_ready, (b - 1) * NG + q + 1, settle=True)
                s_.activation(v_hl[:, 0, GT * q:GT * q + GT, :],
                              xall[:, bass.ds(b * (T // P) + GT * q, GT), :], ACT.Copy).then_inc(vh_ready, 1)

            def weights(b, k):
                g, j, lo = cols(k)
                n = b * NS + k
                act.wait_ge(scores_ready, n + 1)
                atleast(act, al_ready, n - RING + 1)
                atleast(act, pv_done, n - RING + 1)
                r = k % RING
                s_.activation(a_ring[:, r, lo:GQ], ps[:, k % 2, lo:GQ], ACT.Sigmoid, scale=0.25)\
                    .then_inc(a_ready, 1)
                s_.activation(hl_ring[:, 0, r, lo:GQ], ps[:, k % 2, lo:GQ], ACT.Sigmoid, scale=0.25)\
                    .then_inc(ah_ready, 1)

            def scale_out(b, g):
                G = b * NG + g
                act.wait_ge(pv_done, b * NS + END[g])
                atleast(act, back_done, G - 1)
                for c in range(DC):
                    s_.activation(o_t[:, g % 2, c, :], ps[:, 2 + 2 * (g % 2) + c, :], ACT.Copy,
                                  scale=bsgn[:, 2, c:c + 1]).then_inc(ot_ready, 1)

            def copy_x1t(G):
                act.wait_ge(x1_turned, G + 1)
                atleast(act, logits_done, G)
                for c in range(DC):
                    s_.activation(x1_t[:, c, :], ps[:, M0 + c, :], ACT.Copy).then_inc(x1t_ready, 1)

            def gates(G):
                act.wait_ge(below_ready, G + 1)
                atleast(act, gate_ready, G)
                s_.activation(sg[:, 0, :, :], below[:, :, :], ACT.Sigmoid).then_inc(sg_ready, 1)
                s_.activation(sg[:, 1, :, :], below[:, :, :], ACT.Sigmoid, scale=-1.0).then_inc(sg_ready, 1)

            def high_weights(R, n):
                e, s, p = R * U + n, n % U, n % 2
                act.wait_ge(raw_in[s], 48 * (R + n // U + 1))
                atleast(act, gu_done, FC * (e - 1))
                atleast(act, wl_ready, e - 1)
                s_.activation(w_h[:, p, :, :], raw[:, s, 0:4, :], ACT.Copy).then_inc(wh_ready, 1)

            def batch(b, first, last):
                for k in range(NS + 1):
                    if k < NS:
                        weights(b, k)
                    for g in (3, 0, 1, 2):
                        if g == 3 and first:
                            continue
                        bb = b - 1 if g == 3 else b
                        if k == SCALE[g]:
                            scale_out(bb, g)
                        if k == COPY[g]:
                            copy_x1t(bb * NG + g)
                        if k == PLACE[g]:
                            gates(bb * NG + g)
                    for q in range(NG):
                        if q < 2 and last:
                            continue
                        bb = b + 1 if q < 2 else b
                        if k == PREP[q]:
                            signs(bb, q)
                        if k == VHIGH[q]:
                            values_high(bb, q)
                    if last and k in (NS - 4, NS - 2):
                        act.wait_ge(pv_done, (B - 1) * NS + OFF[3] + 2 * GT)
                        high_weights(0, (k - NS + 4) // 2)

            signs(0, 0)
            values_high(0, 0)
            signs(0, 1)
            values_high(0, 1)
            batch(0, True, False)
            with act.Fori(1, B - 1) as b:
                batch(b, False, False)
            batch(B - 1, False, True)
            scale_out(B - 1, 3)
            copy_x1t(B * NG - 1)
            gates(B * NG - 1)

            def high_x(R, n):
                e, p = R * U + n, n % 2
                act.wait_ge(xs_turned, e + 1)
                atleast(act, gu_done, FC * (e - 1))
                atleast(act, xl_ready, e - 1)
                s_.activation(x_h[:, p, :, :], ps[:, 0:DC, 0:CAP], ACT.Copy).then_inc(xh_ready, 1)

            def silu(R, n, f):
                e = R * U + n
                act.wait_ge(gu_done, FC * e + f + 1)
                atleast(act, h_ready, FC * (e - 1) + f + 1)
                s_.activation(act_s[:, f, :], ps[:, 2 + 2 * f, 0:CAP], ACT.Silu).then_inc(silu_ready, 1)

            def second_norm(R, n):
                e, p = R * U + n, n % 2
                act.wait_ge(zrs_ready, e + 1)
                atleast(act, os_out[p], 16 * CT * (R * (U // 2) + n // 2))
                for t in range(CT):
                    rows = P if t < CFULL else CREST
                    s_.activation(o_s[0:rows, p, t, :], z[0:rows, p, t, :], ACT.Identity,
                                  bias=zrs[0:rows, p, 2, t:t + 1], scale=zrs[0:rows, p, 1, t:t + 1])\
                        .then_inc(os_ready, 1)

            def turn(R, n, ahead=True):
                if ahead and n >= 1:
                    high_weights(R, n + 1)
                silu(R, n, 0)
                if ahead:
                    high_x(R, n + 1)
                if n >= 2:
                    second_norm(R, n - 2)
                silu(R, n, 1)

            for par in range(2):
                act.wait_ge(alone_out[par], 16 * B * NG // 2)
            high_x(0, 0)
            turn(0, 0)
            turn(0, 1)
            with act.Fori(0, (E - 4) // U) as R:
                for n in range(2, 2 + U):
                    turn(R, n)
            RL = (E - 4) // U
            turn(RL, 2)
            turn(RL, 3, ahead=False)
            second_norm(RL, 2)
            second_norm(RL, 3)

        @block.tensor
        def _(pe):
            mm = nc.tensor.matmul

            def scores(b, k):
                g, j, lo = cols(k)
                n = b * NS + k
                if j == 0:
                    pe.wait_ge(kt_ready, DC * (b * NG + g + 1))
                atleast(pe, ah_ready, n - 1)
                o = ps[:, k % 2, lo:GQ]
                diag = j >= GT * g
                for c in range(DC):
                    last = mm(o, k_t[:, c, j * P:(j + 1) * P], q_t[:, c, g * GQ + lo:(g + 1) * GQ],
                              start=(c == 0), stop=(c == DC - 1 and not diag))
                if diag:
                    last = mm(ps[:, k % 2, lo:lo + P], identb[:, :], maskb[:, :], start=False, stop=True)
                last.then_inc(scores_ready, 1)

            def values(b, k):
                g, j, lo = cols(k)
                n = b * NS + k
                r = k % RING
                if j == 0:
                    atleast(pe, v_ready, b * NG + g + 1)
                    atleast(pe, ot_ready, DC * (b * NG + g - 1))
                pe.wait_ge(ah_ready, n + 1)
                pe.wait_ge(al_ready, n + 1)
                for c in range(DC):
                    o = ps[:, 2 + 2 * (g % 2) + c, lo:GQ]
                    vh = v_hl[:, 0, j, c * P:(c + 1) * P]
                    vl = v_hl[:, 1, j, c * P:(c + 1) * P]
                    end = j == GT * g + GT - 1
                    mm(o, vh, hl_ring[:, 0, r, lo:GQ], start=(j == 0), stop=False)
                    mm(o, vh, hl_ring[:, 1, r, lo:GQ], start=False, stop=False)
                    last = mm(o, vl, hl_ring[:, 0, r, lo:GQ], start=False, stop=end)
                last.then_inc(pv_done, 1)

            def turn_signs(b, q):
                n = b * NG + q
                pe.wait_ge(sgn_ready, n + 1)
                o = ps[:, M1, :].bitcast(BF16).rearrange("p (c t) -> p c t", c=DC)
                for c in range(DC):
                    for i in range(GT):
                        last = nc.tensor.transpose(o[:, c, i * P:(i + 1) * P], sgn[:, i, c * P:(c + 1) * P],
                                                   identb[:, :])
                last.then_inc(sgn_turned, 1)

            def back(G, par):
                pe.wait_ge(ot_ready, DC * (G + 1))
                o = ps[:, M0:M1 + 1, :].rearrange("p a (i d) -> p (a i) d", d=D)
                for i in range(GT):
                    for c in range(DC):
                        last = nc.tensor.transpose(o[:, i, c * P:(c + 1) * P],
                                                   o_t[:, par, c, i * P:(i + 1) * P], ident[:, :])
                last.then_inc(back_done, 1)

            def turn_x1(G, par):
                pe.wait_ge(x1_ready, (G + 1) * GT)
                for i in range(GT):
                    for c in range(DC):
                        last = nc.tensor.transpose(ps[:, M0 + c, i * P:(i + 1) * P],
                                                   xrow[:, par, i, c * P:(c + 1) * P], ident[:, :])
                last.then_inc(x1_turned, 1)

            def router(G):
                pe.wait_ge(x1t_ready, DC * (G + 1))
                for i in range(GT):
                    for c in range(DC):
                        last = mm(ps[:, M0, i * E:(i + 1) * E], x1_t[:, c, i * P:(i + 1) * P], w_r[:, c, :],
                                  start=(c == 0), stop=(c == DC - 1))
                last.then_inc(logits_done, 1)

            def counts(G):
                pe.wait_ge(hot_ready, G + 1)
                pe.wait_ge(seen_ready, G + 1)
                for i in range(GT):
                    o = ps[:, M1, i * E:(i + 1) * E]
                    mm(o, tri[:, :], hot[:, i, :], start=True, stop=False)
                    for h in range(i):
                        mm(o, onesb[:, :], hot[:, h, :], start=False, stop=False)
                    last = mm(o, onesb[:, :], seen[:, :], start=False, stop=True)
                last.then_inc(counts_done, 1)

            def batch(b, first, last):
                for k in range(NS):
                    if k + 2 < NS:
                        scores(b, k + 2)
                    elif not last:
                        scores(b + 1, k + 2 - NS)
                    values(b, k)
                    for g in (3, 0, 1, 2):
                        if g == 3 and first:
                            continue
                        G = (b - 1 if g == 3 else b) * NG + g
                        prepared = b * NG + 2 + sum(PREP[q] < k for q in (2, 3, 0, 1))
                        if last:
                            prepared = min(prepared, B * NG)
                        if k == BACK[g]:
                            atleast(pe, lg_ready, G - (1 if g == 0 else 0))
                            atleast(pe, pos_read, G - (1 if g == 0 else 0))
                            pe.wait_ge(qt_ready, prepared)
                            back(G, g % 2)
                        if k == TURN[g]:
                            pe.wait_ge(res_ready, G + (2 if g == 3 else 1))
                            atleast(pe, pos_read, G)
                            pe.wait_ge(qt_ready, prepared)
                            turn_x1(G, g % 2)
                        if k == ROUTE[g]:
                            router(G)
                        if k == COUNT[g]:
                            counts(G)
                    for q in range(NG):
                        if k == PREP[q] and not (q < 2 and last):
                            bb = b + 1 if q < 2 else b
                            atleast(pe, res_ready, b * NG + {2: 0, 3: 1, 0: 3, 1: 3}[q])
                            atleast(pe, pos_read, b * NG + {2: -1, 3: 0, 0: 2, 1: 2}[q])
                            atleast(pe, qt_ready, bb * NG + q)
                            turn_signs(bb, q)

            pe.wait_ge(consts, 9)
            turn_signs(0, 0)
            pe.wait_ge(qt_ready, 1)
            turn_signs(0, 1)
            scores(0, 0)
            scores(0, 1)
            batch(0, True, False)
            with pe.Fori(1, B - 1) as b:
                batch(b, False, False)
            batch(B - 1, False, True)
            G = B * NG - 1
            pe.wait_ge(lg_ready, G)
            pe.wait_ge(pos_read, G)
            back(G, 1)
            pe.wait_ge(res_ready, G + 1)
            turn_x1(G, 1)
            router(G)
            counts(G)

            def turn_x(R, n):
                e, s = R * U + n, n % U
                pe.wait_ge(xs_in[s], 32 * (R + n // U + 1))
                atleast(pe, xh_ready, e)
                atleast(pe, xl_ready, e)
                for c in range(DC):
                    for t in range(CT):
                        m = P if t < CFULL else CREST
                        last = nc.tensor.transpose(ps[:, c, t * P:t * P + m], xs[0:m, s, t, c * P:(c + 1) * P],
                                                   ident[0:m, 0:m])
                last.then_inc(xs_turned, 1)

            def gate_up(R, n, f):
                e, p = R * U + n, n % 2
                if f == 0:
                    pe.wait_ge(wl_ready, e + 1)
                    pe.wait_ge(xh_ready, e + 1)
                    pe.wait_ge(xl_ready, e + 1)
                atleast(pe, h_ready, FC * (e - 1) + f + 1)
                for u in range(2):
                    o = ps[:, 2 + 2 * f + u, 0:CAP]
                    for c in range(DC):
                        wh = w_h[:, p, 2 * u + c, f * P:(f + 1) * P]
                        wl = w_l[:, p, 2 * u + c, f * P:(f + 1) * P]
                        mm(o, wh, x_h[:, p, c, :], start=(c == 0), stop=False)
                        mm(o, wh, x_l[:, p, c, :], start=False, stop=False)
                        last = mm(o, wl, x_h[:, p, c, :], start=False, stop=(c == DC - 1))
                last.then_inc(gu_done, 1)

            def down(R, n):
                e, s, p = R * U + n, n % U, n % 2
                pe.wait_ge(h_ready, FC * (e + 1))
                pe.wait_ge(raw_in[s], 48 * (R + n // U + 1))
                atleast(pe, z_step, e * CT)
                for t in range(CT):
                    m = P if t < CFULL else CREST
                    o = ps[0:m, 6 + t // 2, (t % 2) * D:(t % 2 + 1) * D]
                    for f in range(FC):
                        last = mm(o, act_h[:, p, f, t * P:t * P + m], raw[:, s, 4 + f, :], start=(f == 0),
                                  stop=(f == FC - 1))
                    last.then_inc(y_done, 1)

            def turn(R, n, ahead=True):
                gate_up(R, n, 0)
                if ahead:
                    turn_x(R, n + 1)
                if n >= 1:
                    down(R, n - 1)
                gate_up(R, n, 1)

            pe.wait_ge(lg_ready, B * NG)
            pe.wait_ge(pos_read, B * NG)
            turn_x(0, 0)
            turn(0, 0)
            turn(0, 1)
            with pe.Fori(0, (E - 4) // U) as R:
                for n in range(2, 2 + U):
                    turn(R, n)
            RL = (E - 4) // U
            turn(RL, 2)
            turn(RL, 3, ahead=False)
            down(RL, 3)

        @block.vector
        def _(dve):
            v_ = nc.vector
            dve.wait_ge(bsgn_ready, 1)
            v_.tensor_tensor(qk_sgn[:, :], bsgn[:, 0, :], bsgn[:, 1, :], ALU.mult).then_inc(qksgn_ready, 1)
            v_.memset(seen[:, :], 0.0).then_inc(seen_ready, 1)
            dve.wait_ge(qksgn_ready, 1)
            dve.wait_ge(consts, 9)

            def queries_keys(b, q):
                n = b * NG + q
                dve.wait_ge(sgn_turned, n + 1)
                o = ps[:, M1, :].bitcast(BF16).rearrange("p (c t) -> p c t", c=DC)
                sl = slice(q * GQ, (q + 1) * GQ)
                v_.tensor_copy(q_t[:, :, sl], o).then_inc(qt_ready, 1)
                dve.wait_ge(qt_ready, n + 1)
                for c in range(DC):
                    v_.tensor_scalar(k_t[:, c, sl], q_t[:, c, sl], qk_sgn[:, c:c + 1], None, ALU.mult)\
                        .then_inc(kt_ready, 1)

            def low(b, k):
                g, j, lo = cols(k)
                n = b * NS + k
                r = k % RING
                dve.wait_ge(a_ready, n + 1)
                dve.wait_ge(ah_ready, n + 1)
                atleast(dve, pv_done, n - RING + 1)
                v_.tensor_tensor(hl_ring[:, 1, r, lo:GQ], a_ring[:, r, lo:GQ],
                                 hl_ring[:, 0, r, lo:GQ].bitcast(F32), ALU.subtract).then_inc(al_ready, 1)

            def residual(G):
                dve.wait_ge(back_done, G + 1)
                atleast(dve, x1_ready, G * GT)
                v_.tensor_tensor(res[:, :, :], ps[:, M0:M1 + 1, :].rearrange("p a (i d) -> p (a i) d", d=D),
                                 xall[:, bass.ds(G * GT, GT), :], ALU.add).then_inc(res_ready, 1)

            def statistics(G, part):
                dve.wait_ge(res_ready, G + 1)
                for i in ((0, 1, 2), (3,))[part]:
                    v_.bn_stats(stats[:, i, :], res[:, i, :]).then_inc(stats_step, 1)
                if part == 1:
                    dve.wait_ge(stats_step, (G + 1) * GT)
                    atleast(dve, rstd_step, G * 6, settle=True)
                    for i in range(GT):
                        v_.bn_aggr(mv[:, i, :], stats[:, i, :]).then_inc(mv_ready, 1)

            def normalise(G, turn, par):
                dve.wait_ge(rstd_step, G * 6 + 2)
                dve.wait_ge(mv_ready, (G + 1) * GT)
                atleast(dve, scattered[par], turn * 16 * GT)
                for i in range(GT):
                    v_.tensor_scalar(xrow[:, par, i, 0:D], res[:, i, :], mv[:, i, 0:1], small[:, 1, i:i + 1],
                                     ALU.subtract, ALU.mult).then_inc(x1_ready, 1)

            SN = 13

            def pick(G, part):
                base = G * SN
                if part == 0:
                    dve.wait_ge(logits_done, G + 1)
                    v_.tensor_copy(lg[:, :, :], ps[:, M0, 0:GT * E].rearrange("p (i e) -> p i e", e=E))\
                        .then_inc(lg_ready, 1)
                    atleast(dve, lg_ready, G + 1, settle=True)
                    for i in range(GT):
                        v_.max(top[:, i, :], lg[:, i, :]).then_inc(route_step, 1)
                    dve.wait_ge(route_step, base + 4)
                    atleast(dve, sg_ready, 2 * G)
                    v_.tensor_tensor(below[:, :, :], lg[:, :, :], top[:, :, 0:1].broadcast_to([P, GT, E]),
                                     ALU.subtract).then_inc(below_ready, 1)
                    return
                atleast(dve, route_step, base + 4, settle=True)
                for i in range(GT):
                    v_.max_index(topi[:, i, :], top[:, i, :], lg[:, i, :]).then_inc(route_step, 1)
                dve.wait_ge(route_step, base + 8)
                v_.tensor_copy(topf[:, :], topi[:, :, 0]).then_inc(route_step, 1)
                dve.wait_ge(route_step, base + 9)
                v_.tensor_tensor(hot[:, :, :], iota_e[:, :, :],
                                 topf[:, :].unsqueeze(2).broadcast_to([P, GT, E]), ALU.is_equal)\
                    .then_inc(hot_ready, 1)

            def place(G, par):
                base = G * SN + 9
                dve.wait_ge(counts_done, G + 1)
                v_.tensor_tensor(pm[:, :, :], hot[:, :, :],
                                 ps[:, M1, 0:GT * E].rearrange("p (i e) -> p i e", e=E), ALU.mult)\
                    .then_inc(pos_read, 1)
                v_.tensor_reduce(hots[:, :], hot[:, :, :].rearrange("p i e -> p e i"), AX_X, ALU.add)\
                    .then_inc(route_step, 1)
                dve.wait_ge(pos_read, G + 1)
                v_.tensor_reduce(rt[:, 0, :], pm[:, :, :], AX_X, ALU.add).then_inc(route_step, 1)
                dve.wait_ge(route_step, base + 1)
                v_.tensor_tensor(seen[:, :], seen[:, :], hots[:, :], ALU.add).then_inc(seen_ready, 1)
                dve.wait_ge(route_step, base + 2)
                v_.tensor_scalar(rt[:, 1, :], rt[:, 0, :], CAP + 0.5, SKIP, ALU.is_gt, ALU.mult)\
                    .then_inc(route_step, 1)
                v_.scalar_tensor_tensor(out=rt[:, 2, :], in0=topf[:, :], scalar=float(CAP), in1=rt[:, 0, :],
                                        op0=ALU.mult, op1=ALU.add).then_inc(route_step, 1)
                dve.wait_ge(route_step, base + 4)
                v_.scalar_tensor_tensor(out=slot[:, par, :], in0=rt[:, 2, :], scalar=-1.0, in1=rt[:, 1, :],
                                        op0=ALU.add, op1=ALU.add).then_inc(slot_ready, 1)

            def gate(G, par):
                dve.wait_ge(sg_ready, 2 * G + 2)
                v_.reciprocal(quot[:, :, :], sg[:, 1, :, :]).then_inc(gate_step, 1)
                dve.wait_ge(gate_step, 4 * G + 1)
                v_.tensor_tensor(quot[:, :, :], quot[:, :, :], sg[:, 0, :, :], ALU.mult).then_inc(gate_step, 1)
                dve.wait_ge(gate_step, 4 * G + 2)
                v_.tensor_reduce(rt[:, 3, :], quot[:, :, :], AX_X, ALU.add).then_inc(gate_step, 1)
                dve.wait_ge(gate_step, 4 * G + 3)
                v_.reciprocal(rt[:, 4, :], rt[:, 3, :]).then_inc(gate_step, 1)
                dve.wait_ge(gate_step, 4 * G + 4)
                v_.tensor_scalar(xrow[:, par, :, D], rt[:, 4, :], 0.5, None, ALU.mult).then_inc(gate_ready, 1)

            def low_weights(R, n):
                e, s, p = R * U + n, n % U, n % 2
                dve.wait_ge(wh_ready, e + 1)
                v_.tensor_tensor(w_l[:, p, :, :], raw[:, s, 0:4, :], w_h[:, p, :, :].bitcast(F32),
                                 ALU.subtract).then_inc(wl_ready, 1)

            def batch(b, first, last):
                for k in range(NS + 1):
                    if k < NS:
                        low(b, k)
                    for g in (3, 0, 1, 2):
                        if g == 3 and first:
                            continue
                        G = (b - 1 if g == 3 else b) * NG + g
                        turn = 2 * b + {3: -1, 0: 0, 1: 0, 2: 1}[g]
                        if k == SUM[g]:
                            residual(G)
                        if k in (STATS[g], STATS[g] + 1):
                            statistics(G, k - STATS[g])
                        if k == NORM[g]:
                            normalise(G, turn, g % 2)
                        if k in (PICK[g], PICK[g] + 1):
                            pick(G, k - PICK[g])
                        if k == PLACE[g]:
                            place(G, g % 2)
                        if k == GATE[g]:
                            gate(G, g % 2)
                    for q in range(NG):
                        if k == QK[q] and not (q < 2 and last):
                            queries_keys(b + 1 if q < 2 else b, q)
                if last:
                    low_weights(0, 0)
                    low_weights(0, 1)

            queries_keys(0, 0)
            queries_keys(0, 1)
            batch(0, True, False)
            with dve.Fori(1, B - 1) as b:
                batch(b, False, False)
            batch(B - 1, False, True)
            G = B * NG - 1
            residual(G)
            statistics(G, 0)
            statistics(G, 1)
            normalise(G, 2 * B - 1, 1)
            pick(G, 0)
            pick(G, 1)
            place(G, 1)
            gate(G, 1)

            v_.memset(zmv[:, :, :, :], 0.0).then_inc(zmv_clear, 1)
            dve.wait_ge(zmv_clear, 1)
            def low_x(R, n):
                e, p = R * U + n, n % 2
                dve.wait_ge(xh_ready, e + 1)
                atleast(dve, gu_done, FC * (e - 1))
                v_.tensor_tensor(x_l[:, p, :, :], ps[:, 0:DC, 0:CAP], x_h[:, p, :, :].bitcast(F32),
                                 ALU.subtract).then_inc(xl_ready, 1)

            def hidden(R, n, f):
                e, p = R * U + n, n % 2
                dve.wait_ge(silu_ready, FC * e + f + 1)
                atleast(dve, y_done, (e - 1) * CT)
                v_.tensor_tensor(act_h[:, p, f, :], act_s[:, f, :], ps[:, 3 + 2 * f, 0:CAP], ALU.mult)\
                    .then_inc(h_ready, 1)

            def combine(R, n):
                e, s, p = R * U + n, n % U, n % 2
                atleast(dve, os_ready, (e - 1) * CT)
                dve.wait_ge(xs_in[s], 32 * (R + n // U + 1))
                for t in range(CT):
                    rows = P if t < CFULL else CREST
                    dve.wait_ge(y_done, e * CT + min(CT, t // 2 * 2 + 2))
                    v_.scalar_tensor_tensor(out=z[0:rows, p, t, :],
                                            in0=ps[0:rows, 6 + t // 2, (t % 2) * D:(t % 2 + 1) * D],
                                            scalar=xs[0:rows, s, t, D:D + 1], in1=xs[0:rows, s, t, 0:D],
                                            op0=ALU.mult, op1=ALU.add).then_inc(z_step, 1)
                for t in range(CT):
                    rows = P if t < CFULL else CREST
                    dve.wait_ge(z_step, e * CT + t + 1)
                    v_.bn_stats(zst[0:rows, t, :], z[0:rows, p, t, :]).then_inc(zst_step, 1)
                atleast(dve, zrs_ready, e - 1, settle=True)
                for t in range(CT):
                    rows = P if t < CFULL else CREST
                    atleast(dve, zst_step, e * CT + t + 1, settle=True)
                    v_.bn_aggr(zmv[0:rows, p, t, :], zst[0:rows, t, :]).then_inc(zmv_ready, 1)

            def turn(R, n, ahead=True):
                hidden(R, n, 0)
                if ahead:
                    low_x(R, n + 1)
                if ahead and n >= 1:
                    low_weights(R, n + 1)
                if n >= 1:
                    combine(R, n - 1)
                hidden(R, n, 1)

            low_x(0, 0)
            turn(0, 0)
            turn(0, 1)
            with dve.Fori(0, (E - 4) // U) as R:
                for n in range(2, 2 + U):
                    turn(R, n)
            RL = (E - 4) // U
            turn(RL, 2)
            turn(RL, 3, ahead=False)
            combine(RL, 3)


_INS = ["L0_attn_x", "L0_attn_bv_q", "L0_attn_bv_k", "L0_attn_bv_v", "L0_ffn_w_router", "L0_ffn_w_gate",
        "L0_ffn_w_up", "L0_ffn_w_down"]
_OUTS = [((4, 2048, 256), "float32")]


def kernel(**inputs):
    import numpy as _np
    import concourse.bacc as _bacc
    from concourse import mybir as _mybir
    from concourse.bass_utils import run_bass_kernel_spmd as _run

    nc = _bacc.Bacc("TRN2", target_bir_lowering=False, num_devices=1)
    arrays, args = {}, []
    for name in _INS:
        a = _np.ascontiguousarray(inputs[name])
        arrays[f"in_{name}_dram"] = a
        args.append(nc.dram_tensor(f"in_{name}_dram", a.shape, _mybir.dt.from_np(a.dtype), kind="ExternalInput").ap())
    for i, (shape, dtype) in enumerate(_OUTS):
        dt = _mybir.dt.from_np(_np.dtype(dtype))
        args.append(nc.dram_tensor(f"out_{i}_dram", shape, dt, kind="ExternalOutput").ap())
    bass_postln_attn_moe_kernel(nc, *args)
    r = _run(nc, [arrays], core_ids=[0])
    got = tuple(r.results[0][f"out_{i}_dram"] for i in range(len(_OUTS)))
    return got[0]
```

```python
from contextlib import ExitStack

import numpy as np

import concourse.bass as bass
from concourse import mybir

ALU = mybir.AluOpType
ACT = mybir.ActivationFunctionType
AX_X = mybir.AxisListType.X
F32 = mybir.dt.float32
F32R = mybir.dt.float32r
BF16 = mybir.dt.bfloat16
U32 = mybir.dt.uint32

P = 128
EPS = 1e-5
MASKED = -30000.0
SKIP = 65536.0
NOBODY = 1 << 20

GT = 4
GQ = GT * P
RING = 4

SUM = {0: (2, 3, 4, 4), 1: (10, 11, 12, 12), 2: (22, 23, 24, 24),
       3: (38, 39, 40, 40)}
STATS = {3: 1, 0: 6, 1: 15, 2: 26}
NORM = {3: (3, 4), 0: (13, 13), 1: (21, 21), 2: (29, 29)}
TURN = {3: 4, 0: 13, 1: 21, 2: 29}
COPY = {3: 6, 0: 15, 1: 23, 2: 31}
ROUTE = {3: 6, 0: 15, 1: 23, 2: 31}
PICK = {3: 8, 0: 17, 1: 25, 2: 33}
COUNT = {3: 9, 0: 18, 1: 26, 2: 34}
EXPS = {3: 9, 0: 18, 1: 26, 2: 34}
PLACE = {3: 11, 0: 20, 1: 28, 2: 36}
GATE = {3: (14, 16), 0: (19, 22), 1: (27, 30), 2: (35, 37)}
AHEAD = (0, 1)
SIGN = {2: 5, 3: 13, 0: 28, 1: 33}
PREP = {2: 6, 3: 15, 0: 31, 1: 34}
QUERY = {2: 7, 3: 16, 0: 32, 1: 37}
KEY = {1: (4, 5), 2: (11, 12), 3: (19, 20), 0: (35, 37)}
VHIGH = {2: 10, 3: 24, 0: 33, 1: 36}


def bass_postln_attn_moe_kernel(nc, x, bv_q, bv_k, bv_v, w_router, w_gate, w_up, w_down, out):
    B, T, D = x.shape
    E, _, F = w_gate.shape
    NT = B * T // P
    NG = T // GQ
    DC, FC = D // P, F // P
    N_TOK = B * T
    CAP = -(-5 * N_TOK // (4 * E))
    ROW = D + 2
    CT = -(-CAP // P)
    CFULL = CAP // P
    CREST = CAP - CFULL * P
    SLOTS = E * CAP
    ZR = 2
    assert NG == 4 and DC == 2 and FC == 2 and NT == 64 and CREST > 0 and E == 32
    STEPS = [(g, j) for g in range(NG) for j in range(GT * g + GT)]
    OFF = [0, 4, 12, 24]
    NS = len(STEPS)
    END = [OFF[g] + GT * g + GT for g in range(NG)]
    U = 4
    assert (E - 4) % U == 0

    out_rows = out.rearrange("b t d -> (b t) d")
    buf = nc.dram_tensor("expert_rows", [SLOTS, ROW], F32)
    buf_rows = buf.ap()

    with ExitStack() as ctx:
        def sb(name, shape, dt):
            return ctx.enter_context(nc.sbuf_tensor(name, shape, dt))

        def sem(name):
            return ctx.enter_context(nc.semaphore(name))

        ps = ctx.enter_context(nc.psum_tensor("ps", [P, 8, 512], F32))
        ident = sb("ident", [P, P], F32)
        identb = sb("identb", [P, P], BF16)
        tri = sb("tri", [P, P], BF16)
        onesb = sb("onesb", [P, P], BF16)
        maskb = sb("maskb", [P, P], BF16)
        iota_e = sb("iota_e", [P, GT, E], F32)
        tok = sb("tok", [P, GT], U32)
        mhalf = sb("mhalf", [P, GT], F32)
        mone = sb("mone", [P, GT], F32)
        bvec = sb("bvec", [P, 2, DC], F32)
        bsgn = sb("bsgn", [P, 2, DC], F32)
        bv_row = sb("bv_row", [P, D], F32)
        qk_sgn = sb("qk_sgn", [P, DC], F32)
        w_r = sb("w_r", [P, DC, E], F32)
        spare = sb("spare", [P, 1], F32)

        xall = sb("xall", [P, NT, D], F32)
        v_hl = sb("v_hl", [P, 2, T // P, D], F32R)
        sgn = sb("sgn", [P, GT, D], BF16)
        q_t = sb("q_t", [P, DC, T], BF16)
        k_t = sb("k_t", [P, DC, T], BF16)
        a_ring = sb("a_ring", [P, RING, GQ], F32)
        hl_ring = sb("hl_ring", [P, 2, RING, GQ], F32R)
        res_even = sb("res", [P, GT, D], F32)
        stats = sb("stats", [P, 2, GT, 6], F32)
        mv = sb("mv", [P, GT, 2], F32)
        small = sb("small", [P, 8, GT], F32)
        xrow = sb("xrow", [P, 2, GT, ROW], F32)
        alone = sb("alone", [P, 2, GT, D], F32)
        x1_t = sb("x1_t", [P, DC, GQ], F32)
        lg = sb("lg", [P, GT, E], F32)
        top = sb("top", [P, GT, 8], F32)
        topi = sb("topi", [P, GT, 8], U32)
        topf = sb("topf", [P, GT], F32)
        hot = sb("hot", [P, GT, E], BF16)
        below = sb("below", [P, GT, E], F32)
        sg = sb("sg", [P, 2, GT, E], F32)
        quot = sb("quot", [P, GT, E], F32)
        pm = sb("pm", [P, GT, E], F32)
        hots = sb("hots", [P, E], F32)
        seen = sb("seen", [P, E], BF16)
        rt = sb("rt", [P, 6, GT], F32)
        slot = sb("slot", [P, 2, GT], U32)

        raw = xall[:, 0:6 * U, :].rearrange("p (s k) f -> p s k f", k=6)
        w_h, w_l = (v_hl[:, n, 0:4 * 2, :].rearrange("p (s k) f -> p s k f", s=2) for n in range(2))
        r_flat = hl_ring[:, :, :, :].rearrange("p a r t -> p (a r t)")
        XN = DC * CAP
        x_h, x_l = (r_flat[:, n * 2 * XN:(n + 1) * 2 * XN].rearrange("p (s k t) -> p s k t", s=2, t=CAP)
                    for n in range(2))
        a_flat = a_ring[:, :, :].rearrange("p r t -> p (r t)")
        HN = FC * CAP
        act_s = a_flat[:, 0:HN].rearrange("p (k t) -> p k t", k=FC)
        act_h = a_flat[:, HN:3 * HN].rearrange("p (s k t) -> p s k t", s=2, t=CAP)
        xs = sb("xs", [P, U, CT, ROW], F32)
        zero = xs[:, 0, :, :].rearrange("p a w -> p (a w)")[:, 0:ZR * ROW]
        RO = CT * ROW
        res_odd = xs[:, :, :, :].rearrange("p s t w -> p (s t w)")[:, RO:RO + GT * D]\
            .rearrange("p (i d) -> p i d", d=D)
        res = (res_even, res_odd)
        z = sb("z", [P, 2, CT, D], F32)
        v_f32 = z[:, :, :, :].rearrange("p a t d -> p (a t) d")[:, 0:GT, :]
        zst = sb("zst", [P, CT, 6], F32)
        zmv = sb("zmv", [P, 2, CT, 2], F32)
        zrs = sb("zrs", [P, 2, 4, CT], F32)
        ids = sb("ids", [P, U, CT], U32)
        o_s = alone[:, :, 0:CT, :]

        x_in = [sem(f"x_in{q}") for q in range(NG)]
        small_in = sem("small_in")
        zero_step = sem("zero_step")
        zero_out = sem("zero_out")
        consts = sem("consts")
        consts_step = sem("consts_step")
        table_ready = sem("table_ready")
        bsgn_ready = sem("bsgn_ready")
        qksgn_ready = sem("qksgn_ready")
        sgn_ready = sem("sgn_ready")
        vs_ready = sem("vs_ready")
        vh_ready = sem("vh_ready")
        v_ready = sem("v_ready")
        sgn_turned = sem("sgn_turned")
        qt_ready = sem("qt_ready")
        kt_ready = sem("kt_ready")
        scores_ready = sem("scores_ready")
        a_ready = sem("a_ready")
        ah_ready = sem("ah_ready")
        al_ready = sem("al_ready")
        pv_done = sem("pv_done")
        res_ready = sem("res_ready")
        stats_step = sem("stats_step")
        mv_ready = sem("mv_ready")
        rstd_step = sem("rstd_step")
        x1_ready = sem("x1_ready")
        x1_turned = sem("x1_turned")
        x1t_ready = sem("x1t_ready")
        logits_done = sem("logits_done")
        lg_ready = sem("lg_ready")
        route_step = sem("route_step")
        hot_ready = sem("hot_ready")
        below_ready = sem("below_ready")
        sg_ready = sem("sg_ready")
        counts_done = sem("counts_done")
        pos_read = sem("pos_read")
        seen_ready = sem("seen_ready")
        gate_step = sem("gate_step")
        gate_ready = sem("gate_ready")
        slot_ready = sem("slot_ready")
        tok_step = sem("tok_step")
        alone_ready = sem("alone_ready")
        alone_out = [sem(f"alone_out{i}") for i in range(2)]
        scattered = [sem(f"scattered{i}") for i in range(2)]

        raw_in = [sem(f"raw_in{i}") for i in range(U)]
        xs_in = [sem(f"xs_in{i}") for i in range(U)]
        xs_turned = sem("xs_turned")
        xh_ready = sem("xh_ready")
        xl_ready = sem("xl_ready")
        wh_ready = sem("wh_ready")
        wl_ready = sem("wl_ready")
        silu_ready = sem("silu_ready")
        h_ready = sem("h_ready")
        gu_done = sem("gu_done")
        y_done = sem("y_done")
        z_step = sem("z_step")
        zst_step = sem("zst_step")
        zmv_clear = sem("zmv_clear")
        zmv_ready = sem("zmv_ready")
        zr_step = sem("zr_step")
        zrs_ready = sem("zrs_ready")
        ids_half = sem("ids_half")
        ids_ready = sem("ids_ready")
        os_ready = sem("os_ready")
        os_out = [sem(f"os_out{i}") for i in range(2)]

        def atleast(eng, s, value, settle=False):
            if isinstance(value, int) and value <= 0:
                return
            if settle and not isinstance(value, int):
                value = eng.to_reg(value)
                eng.wait_ge(consts, 10)
            eng.wait_ge(s, value)

        block = ctx.enter_context(nc.Block())
        M0, M1 = 6, 7

        def cols(k):
            g, j = STEPS[k]
            return g, j, max(0, j - GT * g) * P

        @block.sync
        def _(sp):
            def load_x(b, q):
                src = x[b, q * GQ:(q + 1) * GQ, :].rearrange("(i p) d -> p i d", p=P)
                sp.dma_start(xall[:, bass.ds(b * (T // P) + GT * q, GT), :], src).then_inc(x_in[q], 16)

            load_x(0, 0)
            for n, v in enumerate((bv_q, bv_k)):
                sp.dma_start(bvec[:, n, :], v.rearrange("(c p) -> p c", p=P),
                             allow_slow_non_contiguous=True).then_inc(small_in, 16)
            sp.dma_start(bv_row[:, :], bv_v.partition_broadcast(P)).then_inc(small_in, 16)
            sp.dma_start(w_r[:, :, :], w_router.rearrange("(c p) e -> p c e", p=P)).then_inc(small_in, 16)
            for q in range(1, NG):
                load_x(0, q)
            sp.wait_ge(zero_step, 3)
            zrows = buf_rows.rearrange("(n p r) w -> n p (r w)", p=P, r=ZR)
            for n in range(SLOTS // (P * ZR)):
                sp.dma_start(zrows[n], zero).then_inc(zero_out, 16)

            def store_alone(G, par):
                atleast(sp, alone_ready, G + 1)
                dst = out_rows[bass.ds(G * GQ, GQ), :].rearrange("(i p) d -> p i d", p=P)
                sp.dma_start(dst, alone[:, par, :, :]).then_inc(alone_out[par], 16)

            with sp.Fori(1, B) as b:
                for q in range(NG):
                    sp.wait_ge(v_ready, (b - 1) * NG + q + 1)
                    sp.wait_ge(sgn_ready, (b - 1) * NG + q + 1)
                    load_x(b, q)
                    store_alone((b - 1) * NG + q, q % 2)

            def load_raw(e, s):
                for n, w in enumerate((w_gate, w_up, w_down)):
                    sp.dma_start(raw[:, s, 2 * n:2 * n + 2, :],
                                 w[e].rearrange("(c p) f -> p c f", p=P)).then_inc(raw_in[s], 16)

            def load_xs(e, s):
                rows = buf_rows[bass.ds(e * CAP, CAP), :]
                sp.dma_start(xs[:, s, 0:CFULL, :],
                             rows[0:CFULL * P, :].rearrange("(i p) w -> p i w", p=P)).then_inc(xs_in[s], 16)
                sp.dma_start(xs[0:CREST, s, CFULL, :], rows[CFULL * P:CAP, :]).then_inc(xs_in[s], 16)

            last = (B - 1) * NG
            for s in range(U):
                sp.wait_ge(res_ready, 6 * (s + 1))
                load_raw(s, s)
            for q in range(NG):
                store_alone(last + q, q % 2)
            for par in range(2):
                sp.wait_ge(scattered[par], 16 * GT * B * NG // 2)
            for e in range(U):
                load_xs(e, e)

            with sp.Fori(0, (E - U) // U) as R:
                for i in range(U):
                    e = R * U + i
                    sp.wait_ge(z_step, (e + 1) * CT)
                    sp.wait_ge(ids_ready, e + 1)
                    load_xs(e + U, i)
                    sp.wait_ge(wh_ready, e + 1)
                    sp.wait_ge(wl_ready, e + 1)
                    sp.wait_ge(y_done, (e + 1) * CT)
                    load_raw(e + U, i)
            for par in range(2):
                sp.wait_ge(alone_out[par], 16 * B * NG // 2)

        @block.gpsimd
        def _(pool):
            g_ = nc.gpsimd
            g_.memset(zero, 0.0).then_inc(zero_step, 1)
            pool.wait_ge(zero_step, 1)
            g_.memset(zero.rearrange("p (r w) -> p r w", w=ROW)[:, :, D + 1].bitcast(U32), NOBODY)\
                .then_inc(zero_step, 2)
            g_.memset(ident[:, :], 0.0).then_inc(consts_step, 1)
            g_.memset(identb[:, :], 0.0).then_inc(consts_step, 1)
            g_.memset(tri[:, :], 1.0).then_inc(consts_step, 1)
            g_.memset(maskb[:, :], 0.0).then_inc(consts_step, 1)
            g_.memset(onesb[:, :], 1.0).then_inc(consts, 1)
            g_.memset(mhalf[:, :], -0.5).then_inc(consts, 1)
            g_.memset(mone[:, :], -1.0).then_inc(consts, 1)
            g_.memset(spare[:, :], 0.0).then_inc(consts, 1)
            pool.wait_ge(consts_step, 4)
            for m in (ident, identb):
                g_.affine_select(out=m[:, :], in_=m[:, :], compare_op=ALU.not_equal, fill=1.0, base=0,
                                 pattern=[[-1, P]], channel_multiplier=1).then_inc(consts, 1)
            g_.affine_select(out=tri[:, :], in_=tri[:, :], compare_op=ALU.is_ge, fill=0.0, base=0,
                             pattern=[[1, P]], channel_multiplier=-1).then_inc(consts, 1)
            g_.affine_select(out=maskb[:, :], in_=maskb[:, :], compare_op=ALU.is_ge, fill=MASKED, base=0,
                             pattern=[[1, P]], channel_multiplier=-1).then_inc(consts, 1)
            g_.iota(iota_e[:, :, :], pattern=[[0, GT], [1, E]], base=0, channel_multiplier=0,
                    allow_small_or_imprecise_dtypes=True).then_inc(consts, 1)
            g_.iota(tok[:, :], pattern=[[P, GT]], base=0, channel_multiplier=1,
                    allow_small_or_imprecise_dtypes=True).then_inc(consts, 1)

            def values_signed(b, q):
                atleast(pool, x_in[q], (b + 1) * 16, settle=True)
                atleast(pool, v_ready, b * NG + q, settle=True)
                g_.tensor_tensor(v_f32, xall[:, bass.ds(b * (T // P) + GT * q, GT), :],
                                 bv_row[:, :].unsqueeze(1).broadcast_to([P, GT, D]), ALU.mult).then_inc(vs_ready, 1)

            def values_low(b, q):
                sl = slice(GT * q, GT * q + GT)
                atleast(pool, vh_ready, b * NG + q + 1, settle=True)
                g_.tensor_tensor(v_hl[:, 1, sl, :], v_f32, v_hl[:, 0, sl, :].bitcast(F32), ALU.subtract)\
                    .then_inc(v_ready, 1)

            RN = 6

            def rstd(G, par):
                atleast(pool, mv_ready, (G + 1) * GT, settle=True)
                atleast(pool, alone_ready, G, settle=True)
                base = G * RN
                atleast(pool, x1_ready, G * GT, settle=True)
                var = mv[:, :, 1]
                g_.tensor_scalar(small[:, 0, :], var, EPS, None, ALU.add).then_inc(rstd_step, 1)
                atleast(pool, rstd_step, base + 1, settle=True)
                g_.tensor_tensor(small[:, 1, :], small[:, 0, :], mhalf[:, :], ALU.pow).then_inc(rstd_step, 1)
                atleast(pool, rstd_step, base + 2, settle=True)
                g_.tensor_tensor(small[:, 2, :], var, small[:, 1, :], ALU.mult).then_inc(rstd_step, 1)
                atleast(pool, rstd_step, base + 3, settle=True)
                g_.tensor_tensor(small[:, 3, :], small[:, 2, :], small[:, 1, :], ALU.mult).then_inc(rstd_step, 1)
                atleast(pool, rstd_step, base + 4, settle=True)
                g_.tensor_scalar(small[:, 4, :], small[:, 3, :], EPS / 4, None, ALU.add).then_inc(rstd_step, 1)
                atleast(pool, rstd_step, base + 5, settle=True)
                g_.tensor_tensor(small[:, 5, :], small[:, 4, :], mhalf[:, :], ALU.pow).then_inc(rstd_step, 1)

            def rows_alone(G, half, par):
                atleast(pool, rstd_step, G * RN + RN, settle=True)
                atleast(pool, x1_ready, (G + 1) * GT, settle=True)
                atleast(pool, alone_out[par], half * 16, settle=True)
                g_.tensor_tensor(alone[:, par, :, :], xrow[:, par, :, 0:D],
                                 small[:, 5, :].unsqueeze(2).broadcast_to([P, GT, D]), ALU.mult)\
                    .then_inc(alone_ready, 1)
                g_.tensor_copy(xrow[:, par, :, D + 1].bitcast(U32), tok[:, :]).then_inc(tok_step, 1)
                atleast(pool, tok_step, G * 2 + 1, settle=True)
                g_.tensor_scalar(tok[:, :], tok[:, :], float(GQ), None, ALU.add).then_inc(tok_step, 1)
                atleast(pool, tok_step, G * 2 + 2, settle=True)

            def scatter(G, par):
                atleast(pool, gate_ready, G + 1, settle=True)
                atleast(pool, slot_ready, G + 1, settle=True)
                for i in range(GT):
                    g_.indirect_dma_start(
                        out=buf_rows, out_offset=bass.IndirectOffsetOnAxis(ap=slot[:, par, i:i + 1], axis=0),
                        in_=xrow[:, par, i, :], in_offset=None, bounds_check=SLOTS - 1,
                        oob_is_err=False).then_inc(scattered[par], 16)

            def batch(b, first, last):
                n = b * NG
                if not first:
                    rstd(n - 1, 1)
                    rows_alone(n - 1, 2 * b - 1, 1)
                rstd(n, 0)
                values_signed(b, 2)
                values_low(b, 2)
                rows_alone(n, 2 * b, 0)
                if not first:
                    scatter(n - 1, 1)
                rstd(n + 1, 1)
                values_signed(b, 3)
                if first:
                    pool.wait_ge(zero_out, 16 * (SLOTS // (P * ZR)))
                rows_alone(n + 1, 2 * b, 1)
                scatter(n, 0)
                rstd(n + 2, 0)
                values_low(b, 3)
                if not last:
                    values_signed(b + 1, 0)
                rows_alone(n + 2, 2 * b + 1, 0)
                scatter(n + 1, 1)
                if not last:
                    values_low(b + 1, 0)
                    values_signed(b + 1, 1)
                scatter(n + 2, 0)
                if not last:
                    values_low(b + 1, 1)

            pool.wait_ge(consts, 10)
            pool.wait_ge(bsgn_ready, 2)
            values_signed(0, 0)
            pool.wait_ge(v_ready, 1)
            values_signed(0, 1)
            values_low(0, 1)
            batch(0, True, False)
            with pool.Fori(1, B - 1) as b:
                batch(b, False, False)
            batch(B - 1, False, True)
            last = (B - 1) * NG

            def numbers(R, n):
                e, p = R * U + n, n % 2
                atleast(pool, xs_in[n % U], 32 * (R + n // U + 1), settle=True)
                if n // 2 > 1 or not isinstance(R, int) or R > 0:
                    atleast(pool, os_out[p], 16 * CT * (R * (U // 2) + n // 2 - 1), settle=True)
                for t, rows in ((slice(0, CFULL), P), (slice(CFULL, CT), CREST)):
                    g_.tensor_copy(ids[0:rows, n % U, t], xs[0:rows, n % U, t, D + 1].bitcast(U32))\
                        .then_inc(ids_half, 1)
                atleast(pool, ids_half, 2 * e + 2, settle=True)
                pool.sem_inc(ids_ready, 1)

            def second_rstd(R, n):
                e, p = R * U + n, n % 2
                atleast(pool, zmv_ready, (e + 1) * CT, settle=True)
                g_.tensor_scalar(zrs[:, p, 0, :], zmv[:, p, :, 1], EPS / 4, None, ALU.add).then_inc(zr_step, 1)
                g_.tensor_tensor(zrs[:, p, 3, :], zmv[:, p, :, 0], mone[:, 0:CT], ALU.mult).then_inc(zr_step, 1)
                atleast(pool, zr_step, 3 * e + 2, settle=True)
                g_.tensor_tensor(zrs[:, p, 1, :], zrs[:, p, 0, :], mhalf[:, 0:CT], ALU.pow)\
                    .then_inc(zr_step, 1)
                atleast(pool, zr_step, 3 * e + 3, settle=True)
                g_.tensor_tensor(zrs[:, p, 2, :], zrs[:, p, 3, :], zrs[:, p, 1, :], ALU.mult)\
                    .then_inc(zrs_ready, 1)

            def store(R, n, tiles=range(CT)):
                e, p = R * U + n, n % 2
                atleast(pool, ids_ready, e + 1, settle=True)
                for t in tiles:
                    atleast(pool, os_ready, e * CT + t + 1, settle=True)
                    rows = P if t < CFULL else CREST
                    g_.indirect_dma_start(
                        out=out_rows, out_offset=bass.IndirectOffsetOnAxis(ap=ids[0:rows, n % U, t:t + 1], axis=0),
                        in_=o_s[0:rows, p, t, :], in_offset=None, bounds_check=N_TOK - 1,
                        oob_is_err=False).then_inc(os_out[p], 16)

            rstd(last + 3, 1)
            rows_alone(last + 3, 2 * B - 1, 1)
            scatter(last + 3, 1)
            for par in range(2):
                pool.wait_ge(alone_out[par], 16 * B * NG // 2)

            def turn(R, n):
                if n >= 3:
                    store(R, n - 3, range(1))
                if n >= 2:
                    second_rstd(R, n - 2)
                numbers(R, n)
                if n >= 3:
                    store(R, n - 3, range(1, CT))

            turn(0, 0)
            turn(0, 1)
            turn(0, 2)
            with pool.Fori(0, (E - 4) // U) as R:
                for n in range(3, 3 + U):
                    turn(R, n)
            RL = (E - 4) // U
            turn(RL, 3)
            store(RL, 1, range(1))
            second_rstd(RL, 2)
            store(RL, 1, range(1, CT))
            store(RL, 2, range(2))
            second_rstd(RL, 3)
            store(RL, 2, range(2, CT))
            store(RL, 3)
            for par in range(2):
                pool.wait_ge(os_out[par], 16 * CT * E // 2)

        @block.scalar
        def _(act):
            s_ = nc.scalar
            act.wait_ge(consts, 10)
            s_.activation(spare[:, :], spare[:, :], ACT.Sigmoid).then_inc(table_ready, 1)
            act.wait_ge(small_in, 64)
            s_.activation(bsgn[:, :, :], bvec[:, :, :], ACT.Sign).then_inc(bsgn_ready, 1)
            s_.activation(bv_row[:, :], bv_row[:, :], ACT.Sign).then_inc(bsgn_ready, 1)
            act.wait_ge(bsgn_ready, 2)

            def signs(b, q):
                act.wait_ge(x_in[q], (b + 1) * 16)
                atleast(act, sgn_turned, b * NG + q)
                s_.activation(sgn[:, :, :], xall[:, bass.ds(b * (T // P) + GT * q, GT), :], ACT.Sign)\
                    .then_inc(sgn_ready, 1)

            def values_high(b, q):
                act.wait_ge(vs_ready, b * NG + q + 1)
                atleast(act, pv_done, (b - 1) * NS + OFF[3] + GT * q + GT)
                s_.activation(v_hl[:, 0, GT * q:GT * q + GT, :], v_f32, ACT.Copy).then_inc(vh_ready, 1)

            def keys(b, q, c):
                n = b * NG + q
                act.wait_ge(qt_ready, n + 1)
                s_.activation(k_t[:, c, q * GQ:(q + 1) * GQ], q_t[:, c, q * GQ:(q + 1) * GQ], ACT.Copy,
                              scale=qk_sgn[:, c:c + 1]).then_inc(kt_ready, 1)

            def weights(b, k):
                g, j, lo = cols(k)
                n = b * NS + k
                act.wait_ge(scores_ready, n + 1)
                atleast(act, al_ready, n - RING + 1)
                atleast(act, pv_done, n - RING + 1)
                r = k % RING
                s_.activation(a_ring[:, r, lo:GQ], ps[:, k % 2, lo:GQ], ACT.Sigmoid, scale=0.25)\
                    .then_inc(a_ready, 1)
                s_.activation(hl_ring[:, 0, r, lo:GQ], ps[:, k % 2, lo:GQ], ACT.Sigmoid, scale=0.25)\
                    .then_inc(ah_ready, 1)

            def copy_x1t(G):
                act.wait_ge(x1_turned, G + 1)
                atleast(act, logits_done, G)
                for c in range(DC):
                    s_.activation(x1_t[:, c, :], ps[:, M0 + c, :], ACT.Copy).then_inc(x1t_ready, 1)

            def gates(G):
                act.wait_ge(below_ready, G + 1)
                atleast(act, gate_ready, G)
                s_.activation(sg[:, 0, :, :], below[:, :, :], ACT.Sigmoid).then_inc(sg_ready, 1)
                s_.activation(sg[:, 1, :, :], below[:, :, :], ACT.Sigmoid, scale=-1.0).then_inc(sg_ready, 1)

            def high_weights(R, n):
                e, s, p = R * U + n, n % U, n % 2
                act.wait_ge(raw_in[s], 48 * (R + n // U + 1))
                atleast(act, gu_done, FC * (e - 1))
                atleast(act, wl_ready, e - 1)
                s_.activation(w_h[:, p, :, :], raw[:, s, 0:4, :], ACT.Copy).then_inc(wh_ready, 1)

            def batch(b, first, last):
                for k in range(NS):
                    weights(b, k)
                    for g in (3, 0, 1, 2):
                        if g == 3 and first:
                            continue
                        bb = b - 1 if g == 3 else b
                        if k == COPY[g]:
                            copy_x1t(bb * NG + g)
                        if k == EXPS[g]:
                            gates(bb * NG + g)
                    if first and k == 3:
                        values_high(0, 1)
                    for q in range(NG):
                        for c in range(DC):
                            if k == KEY[q][c] and not (q == 0 and last):
                                keys(b + 1 if q == 0 else b, q, c)
                        if q in AHEAD and last:
                            continue
                        bb = b + 1 if q in AHEAD else b
                        if k == SIGN[q]:
                            signs(bb, q)
                        if k == VHIGH[q]:
                            values_high(bb, q)
                    if last and k in (NS - 4, NS - 2):
                        act.wait_ge(pv_done, (B - 1) * NS + OFF[3] + 2 * GT)
                        high_weights(0, (k - NS + 4) // 2)

            signs(0, 0)
            signs(0, 1)
            act.wait_ge(qksgn_ready, 1)
            for c in range(DC):
                keys(0, 0, c)
            values_high(0, 0)
            batch(0, True, False)
            with act.Fori(1, B - 1) as b:
                batch(b, False, False)
            batch(B - 1, False, True)
            copy_x1t(B * NG - 1)
            gates(B * NG - 1)
            act.wait_ge(table_ready, 1)
            s_.activation(spare[:, :], spare[:, :], ACT.Silu).then_inc(table_ready, 1)

            def high_x(R, n):
                e, p = R * U + n, n % 2
                act.wait_ge(xs_turned, e + 1)
                atleast(act, gu_done, FC * (e - 1))
                atleast(act, xl_ready, e - 1)
                s_.activation(x_h[:, p, :, :], ps[:, 0:DC, 0:CAP], ACT.Copy).then_inc(xh_ready, 1)

            def silu(R, n, f):
                e = R * U + n
                act.wait_ge(gu_done, FC * e + f + 1)
                atleast(act, h_ready, FC * (e - 1) + f + 1)
                s_.activation(act_s[:, f, :], ps[:, 2 + 2 * f, 0:CAP], ACT.Silu).then_inc(silu_ready, 1)

            def second_norm(R, n):
                e, p = R * U + n, n % 2
                act.wait_ge(zrs_ready, e + 1)
                atleast(act, os_out[p], 16 * CT * (R * (U // 2) + n // 2))
                for t in range(CT):
                    rows = P if t < CFULL else CREST
                    s_.activation(o_s[0:rows, p, t, :], z[0:rows, p, t, :], ACT.Identity,
                                  bias=zrs[0:rows, p, 2, t:t + 1], scale=zrs[0:rows, p, 1, t:t + 1])\
                        .then_inc(os_ready, 1)

            def turn(R, n, ahead=True):
                if ahead and n >= 1:
                    high_weights(R, n + 1)
                silu(R, n, 0)
                if ahead:
                    high_x(R, n + 1)
                if n >= 2:
                    second_norm(R, n - 2)
                silu(R, n, 1)

            for par in range(2):
                act.wait_ge(alone_out[par], 16 * B * NG // 2)
            high_x(0, 0)
            turn(0, 0)
            turn(0, 1)
            with act.Fori(0, (E - 4) // U) as R:
                for n in range(2, 2 + U):
                    turn(R, n)
            RL = (E - 4) // U
            turn(RL, 2)
            turn(RL, 3, ahead=False)
            second_norm(RL, 2)
            second_norm(RL, 3)

        @block.tensor
        def _(pe):
            mm = nc.tensor.matmul

            def keep_warm(n, bank=0, moving=q_t[:, 0, 0:GQ]):
                for _ in range(n):
                    mm(ps[:, bank, 0:moving.shape[-1]], onesb[:, :], moving, start=True, stop=True)

            def scores(b, k):
                g, j, lo = cols(k)
                n = b * NS + k
                if j == 0:
                    pe.wait_ge(qt_ready, b * NG + g + 1)
                if j == GT * g:
                    pe.wait_ge(kt_ready, DC * (b * NG + g + 1))
                atleast(pe, ah_ready, n - 1)
                o = ps[:, k % 2, lo:GQ]
                diag = j >= GT * g
                for c in range(DC):
                    last = mm(o, k_t[:, c, j * P:(j + 1) * P], q_t[:, c, g * GQ + lo:(g + 1) * GQ],
                              start=(c == 0), stop=(c == DC - 1 and not diag))
                if diag:
                    last = mm(ps[:, k % 2, lo:lo + P], identb[:, :], maskb[:, :], start=False, stop=True)
                last.then_inc(scores_ready, 1)

            def values(b, k):
                g, j, lo = cols(k)
                n = b * NS + k
                r = k % RING
                if j == GT * g:
                    atleast(pe, v_ready, b * NG + g + 1)
                pe.wait_ge(ah_ready, n + 1)
                pe.wait_ge(al_ready, n + 1)
                for i in range(lo // P, GT):
                    if j == 0:
                        atleast(pe, res_ready, (b * NG + g - 1) * GT + i + 1)
                    o = ps[:, 2 + i, 0:D]
                    ah = hl_ring[:, 0, r, i * P:(i + 1) * P]
                    al = hl_ring[:, 1, r, i * P:(i + 1) * P]
                    mm(o, ah, v_hl[:, 0, j, :], start=(j == 0), stop=False)
                    mm(o, ah, v_hl[:, 1, j, :], start=False, stop=False)
                    last = mm(o, al, v_hl[:, 0, j, :], start=False, stop=(j == GT * g + i))
                last.then_inc(pv_done, 1)

            def turn_signs(b, q):
                n = b * NG + q
                pe.wait_ge(sgn_ready, n + 1)
                o = ps[:, M1, :].bitcast(BF16).rearrange("p (c t) -> p c t", c=DC)
                for c in range(DC):
                    for i in range(GT):
                        last = nc.tensor.transpose(o[:, c, i * P:(i + 1) * P], sgn[:, i, c * P:(c + 1) * P],
                                                   identb[:, :])
                last.then_inc(sgn_turned, 1)

            def turn_x1(G, par):
                for i in range(GT):
                    pe.wait_ge(x1_ready, G * GT + i + 1)
                    for c in range(DC):
                        last = nc.tensor.transpose(ps[:, M0 + c, i * P:(i + 1) * P],
                                                   xrow[:, par, i, c * P:(c + 1) * P], ident[:, :])
                last.then_inc(x1_turned, 1)

            def router(G):
                pe.wait_ge(x1t_ready, DC * (G + 1))
                for i in range(GT):
                    for c in range(DC):
                        last = mm(ps[:, M0, i * E:(i + 1) * E], x1_t[:, c, i * P:(i + 1) * P], w_r[:, c, :],
                                  start=(c == 0), stop=(c == DC - 1))
                last.then_inc(logits_done, 1)

            def counts(G):
                pe.wait_ge(hot_ready, G + 1)
                pe.wait_ge(seen_ready, G + 1)
                for i in range(GT):
                    o = ps[:, M0, i * E:(i + 1) * E]
                    mm(o, tri[:, :], hot[:, i, :], start=True, stop=False)
                    for h in range(i):
                        mm(o, onesb[:, :], hot[:, h, :], start=False, stop=False)
                    last = mm(o, onesb[:, :], seen[:, :], start=False, stop=True)
                last.then_inc(counts_done, 1)

            def batch(b, first, last):
                for k in range(NS):
                    if k + 2 < NS:
                        scores(b, k + 2)
                    elif not last:
                        scores(b + 1, k + 2 - NS)
                    values(b, k)
                    for g in (3, 0, 1, 2):
                        if g == 3 and first:
                            continue
                        G = (b - 1 if g == 3 else b) * NG + g
                        if k == TURN[g]:
                            prepared = b * NG + 2 + sum(PREP[q] < k for q in (2, 3, 0, 1))
                            if last:
                                prepared = min(prepared, B * NG)
                            atleast(pe, pos_read, G)
                            pe.wait_ge(qt_ready, prepared)
                            turn_x1(G, g % 2)
                        if k == ROUTE[g]:
                            router(G)
                        if k == COUNT[g]:
                            counts(G)
                    for q in range(NG):
                        if k == PREP[q] and not (q in AHEAD and last):
                            bb = b + 1 if q in AHEAD else b
                            atleast(pe, qt_ready, bb * NG + q)
                            turn_signs(bb, q)

            pe.wait_ge(consts, 10)
            keep_warm(26, moving=identb[:, :])
            turn_signs(0, 0)
            keep_warm(12, moving=identb[:, :])
            pe.wait_ge(qt_ready, 1)
            turn_signs(0, 1)
            keep_warm(6, moving=identb[:, :])
            scores(0, 0)
            scores(0, 1)
            keep_warm(2, bank=M0)
            batch(0, True, False)
            with pe.Fori(1, B - 1) as b:
                batch(b, False, False)
            batch(B - 1, False, True)
            G = B * NG - 1
            pe.wait_ge(ah_ready, B * NS)
            keep_warm(14)
            pe.wait_ge(pos_read, G)
            turn_x1(G, 1)
            router(G)
            keep_warm(6)
            counts(G)
            keep_warm(44)

            def turn_x(R, n):
                e, s = R * U + n, n % U
                pe.wait_ge(xs_in[s], 32 * (R + n // U + 1))
                atleast(pe, xh_ready, e)
                atleast(pe, xl_ready, e)
                for c in range(DC):
                    for t in range(CT):
                        m = P if t < CFULL else CREST
                        last = nc.tensor.transpose(ps[:, c, t * P:t * P + m], xs[0:m, s, t, c * P:(c + 1) * P],
                                                   ident[0:m, 0:m])
                last.then_inc(xs_turned, 1)

            def gate_up(R, n, f):
                e, p = R * U + n, n % 2
                if f == 0:
                    pe.wait_ge(wl_ready, e + 1)
                    pe.wait_ge(xh_ready, e + 1)
                    pe.wait_ge(xl_ready, e + 1)
                atleast(pe, h_ready, FC * (e - 1) + f + 1)
                for u in range(2):
                    o = ps[:, 2 + 2 * f + u, 0:CAP]
                    for c in range(DC):
                        wh = w_h[:, p, 2 * u + c, f * P:(f + 1) * P]
                        wl = w_l[:, p, 2 * u + c, f * P:(f + 1) * P]
                        mm(o, wh, x_h[:, p, c, :], start=(c == 0), stop=False)
                        mm(o, wh, x_l[:, p, c, :], start=False, stop=False)
                        last = mm(o, wl, x_h[:, p, c, :], start=False, stop=(c == DC - 1))
                last.then_inc(gu_done, 1)

            def down(R, n):
                e, s, p = R * U + n, n % U, n % 2
                pe.wait_ge(h_ready, FC * (e + 1))
                pe.wait_ge(raw_in[s], 48 * (R + n // U + 1))
                atleast(pe, z_step, e * CT)
                for t in range(CT):
                    m = P if t < CFULL else CREST
                    o = ps[0:m, 6 + t // 2, (t % 2) * D:(t % 2 + 1) * D]
                    for f in range(FC):
                        last = mm(o, act_h[:, p, f, t * P:t * P + m], raw[:, s, 4 + f, :], start=(f == 0),
                                  stop=(f == FC - 1))
                    last.then_inc(y_done, 1)

            def turn(R, n, ahead=True):
                gate_up(R, n, 0)
                if ahead:
                    turn_x(R, n + 1)
                if n >= 1:
                    down(R, n - 1)
                gate_up(R, n, 1)

            pe.wait_ge(lg_ready, B * NG)
            pe.wait_ge(pos_read, B * NG)
            turn_x(0, 0)
            keep_warm(8, bank=M0)
            turn(0, 0)
            turn(0, 1)
            with pe.Fori(0, (E - 4) // U) as R:
                for n in range(2, 2 + U):
                    turn(R, n)
            RL = (E - 4) // U
            turn(RL, 2)
            turn(RL, 3, ahead=False)
            down(RL, 3)

        @block.vector
        def _(dve):
            v_ = nc.vector
            dve.wait_ge(bsgn_ready, 1)
            v_.tensor_tensor(qk_sgn[:, :], bsgn[:, 0, :], bsgn[:, 1, :], ALU.mult).then_inc(qksgn_ready, 1)
            v_.memset(seen[:, :], 0.0).then_inc(seen_ready, 1)
            dve.wait_ge(qksgn_ready, 1)
            dve.wait_ge(consts, 10)

            def queries(b, q):
                n = b * NG + q
                dve.wait_ge(sgn_turned, n + 1)
                o = ps[:, M1, :].bitcast(BF16).rearrange("p (c t) -> p c t", c=DC)
                v_.tensor_copy(q_t[:, :, q * GQ:(q + 1) * GQ], o).then_inc(qt_ready, 1)

            def low(b, k):
                g, j, lo = cols(k)
                n = b * NS + k
                r = k % RING
                dve.wait_ge(a_ready, n + 1)
                dve.wait_ge(ah_ready, n + 1)
                atleast(dve, pv_done, n - RING + 1)
                v_.tensor_tensor(hl_ring[:, 1, r, lo:GQ], a_ring[:, r, lo:GQ],
                                 hl_ring[:, 0, r, lo:GQ].bitcast(F32), ALU.subtract).then_inc(al_ready, 1)

            def residual(G, i, done, par):
                dve.wait_ge(pv_done, done)
                v_.tensor_tensor(res[par][:, i, :], ps[:, 2 + i, 0:D], xall[:, G * GT + i, :], ALU.add)\
                    .then_inc(res_ready, 1)

            def row_statistics(G, i, par):
                dve.wait_ge(res_ready, G * GT + i + 1)
                v_.bn_stats(stats[:, par, i, :], res[par][:, i, :]).then_inc(stats_step, 1)

            def statistics(G, par):
                row_statistics(G, GT - 1, par)
                dve.wait_ge(stats_step, (G + 1) * GT)
                atleast(dve, rstd_step, G * 6, settle=True)
                for i in range(GT):
                    v_.bn_aggr(mv[:, i, :], stats[:, par, i, :]).then_inc(mv_ready, 1)

            def normalise(G, turn, par, tiles=range(GT)):
                dve.wait_ge(rstd_step, G * 6 + 2)
                dve.wait_ge(mv_ready, (G + 1) * GT)
                atleast(dve, scattered[par], turn * 16 * GT)
                for i in tiles:
                    v_.tensor_scalar(xrow[:, par, i, 0:D], res[par][:, i, :], mv[:, i, 0:1], small[:, 1, i:i + 1],
                                     ALU.subtract, ALU.mult).then_inc(x1_ready, 1)

            SN = 13

            def pick(G, part):
                base = G * SN
                if part == 0:
                    dve.wait_ge(logits_done, G + 1)
                    v_.tensor_copy(lg[:, :, :], ps[:, M0, 0:GT * E].rearrange("p (i e) -> p i e", e=E))\
                        .then_inc(lg_ready, 1)
                    atleast(dve, lg_ready, G + 1, settle=True)
                    for i in range(GT):
                        v_.max(top[:, i, :], lg[:, i, :]).then_inc(route_step, 1)
                    dve.wait_ge(route_step, base + 4)
                    atleast(dve, sg_ready, 2 * G)
                    v_.tensor_tensor(below[:, :, :], lg[:, :, :], top[:, :, 0:1].broadcast_to([P, GT, E]),
                                     ALU.subtract).then_inc(below_ready, 1)
                    return
                atleast(dve, route_step, base + 4, settle=True)
                for i in range(GT):
                    v_.max_index(topi[:, i, :], top[:, i, :], lg[:, i, :]).then_inc(route_step, 1)
                dve.wait_ge(route_step, base + 8)
                v_.tensor_copy(topf[:, :], topi[:, :, 0]).then_inc(route_step, 1)
                dve.wait_ge(route_step, base + 9)
                v_.tensor_tensor(hot[:, :, :], iota_e[:, :, :],
                                 topf[:, :].unsqueeze(2).broadcast_to([P, GT, E]), ALU.is_equal)\
                    .then_inc(hot_ready, 1)

            def place(G, par):
                base = G * SN + 9
                dve.wait_ge(counts_done, G + 1)
                v_.tensor_tensor(pm[:, :, :], hot[:, :, :],
                                 ps[:, M0, 0:GT * E].rearrange("p (i e) -> p i e", e=E), ALU.mult)\
                    .then_inc(pos_read, 1)
                v_.tensor_reduce(hots[:, :], hot[:, :, :].rearrange("p i e -> p e i"), AX_X, ALU.add)\
                    .then_inc(route_step, 1)
                dve.wait_ge(pos_read, G + 1)
                v_.tensor_reduce(rt[:, 0, :], pm[:, :, :], AX_X, ALU.add).then_inc(route_step, 1)
                dve.wait_ge(route_step, base + 1)
                v_.tensor_tensor(seen[:, :], seen[:, :], hots[:, :], ALU.add).then_inc(seen_ready, 1)
                dve.wait_ge(route_step, base + 2)
                v_.tensor_scalar(rt[:, 1, :], rt[:, 0, :], CAP + 0.5, SKIP, ALU.is_gt, ALU.mult)\
                    .then_inc(route_step, 1)
                v_.scalar_tensor_tensor(out=rt[:, 2, :], in0=topf[:, :], scalar=float(CAP), in1=rt[:, 0, :],
                                        op0=ALU.mult, op1=ALU.add).then_inc(route_step, 1)
                dve.wait_ge(route_step, base + 4)
                v_.scalar_tensor_tensor(out=slot[:, par, :], in0=rt[:, 2, :], scalar=-1.0, in1=rt[:, 1, :],
                                        op0=ALU.add, op1=ALU.add).then_inc(slot_ready, 1)

            def gate(G, par, part):
                if part == 0:
                    dve.wait_ge(sg_ready, 2 * G + 2)
                    v_.reciprocal(quot[:, :, :], sg[:, 1, :, :]).then_inc(gate_step, 1)
                    dve.wait_ge(gate_step, 4 * G + 1)
                    v_.tensor_tensor(quot[:, :, :], quot[:, :, :], sg[:, 0, :, :], ALU.mult)\
                        .then_inc(gate_step, 1)
                    return
                dve.wait_ge(gate_step, 4 * G + 2)
                v_.tensor_reduce(rt[:, 3, :], quot[:, :, :], AX_X, ALU.add).then_inc(gate_step, 1)
                dve.wait_ge(gate_step, 4 * G + 3)
                v_.reciprocal(rt[:, 4, :], rt[:, 3, :]).then_inc(gate_step, 1)
                dve.wait_ge(gate_step, 4 * G + 4)
                v_.tensor_scalar(xrow[:, par, :, D], rt[:, 4, :], 0.5, None, ALU.mult).then_inc(gate_ready, 1)

            def low_weights(R, n):
                e, s, p = R * U + n, n % U, n % 2
                dve.wait_ge(wh_ready, e + 1)
                v_.tensor_tensor(w_l[:, p, :, :], raw[:, s, 0:4, :], w_h[:, p, :, :].bitcast(F32),
                                 ALU.subtract).then_inc(wl_ready, 1)

            def add_tile(b, g, i):
                residual(b * NG + g, i, b * NS + END[g] - GT + i + 1, g % 2)
                if i > 0:
                    row_statistics(b * NG + g, i - 1, g % 2)

            def batch(b, first, last):
                for k in range(NS):
                    low(b, k)
                    for g in range(NG):
                        for i in range(GT):
                            if k == SUM[g][i]:
                                add_tile(b, g, i)
                            if k + NS == SUM[g][i] and not first:
                                add_tile(b - 1, g, i)
                    for g in (3, 0, 1, 2):
                        if g == 3 and first:
                            continue
                        G = (b - 1 if g == 3 else b) * NG + g
                        turn = 2 * b + {3: -1, 0: 0, 1: 0, 2: 1}[g]
                        if k == STATS[g]:
                            statistics(G, g % 2)
                        for half in range(2):
                            if k == NORM[g][half]:
                                normalise(G, turn, g % 2, range(half * GT // 2, (half + 1) * GT // 2))
                        if k in (PICK[g], PICK[g] + 1):
                            pick(G, k - PICK[g])
                        if k == PLACE[g]:
                            place(G, g % 2)
                        for part in range(2):
                            if k == GATE[g][part]:
                                gate(G, g % 2, part)
                    for q in range(NG):
                        if k == QUERY[q] and not (q in AHEAD and last):
                            queries(b + 1 if q in AHEAD else b, q)

            queries(0, 0)
            queries(0, 1)
            dve.wait_ge(vh_ready, 1)
            v_.tensor_tensor(v_hl[:, 1, 0:GT, :], v_f32, v_hl[:, 0, 0:GT, :].bitcast(F32), ALU.subtract)\
                .then_inc(v_ready, 1)
            batch(0, True, False)
            with dve.Fori(1, B - 1) as b:
                batch(b, False, False)
            batch(B - 1, False, True)
            G = B * NG - 1
            add_tile(B - 1, 3, 2)
            add_tile(B - 1, 3, 3)
            statistics(G, 1)
            low_weights(0, 0)
            normalise(G, 2 * B - 1, 1)
            low_weights(0, 1)
            pick(G, 0)
            pick(G, 1)
            gate(G, 1, 0)
            gate(G, 1, 1)
            place(G, 1)

            v_.memset(zmv[:, :, :, :], 0.0).then_inc(zmv_clear, 1)
            dve.wait_ge(zmv_clear, 1)

            def low_x(R, n):
                e, p = R * U + n, n % 2
                dve.wait_ge(xh_ready, e + 1)
                atleast(dve, gu_done, FC * (e - 1))
                v_.tensor_tensor(x_l[:, p, :, :], ps[:, 0:DC, 0:CAP], x_h[:, p, :, :].bitcast(F32),
                                 ALU.subtract).then_inc(xl_ready, 1)

            def hidden(R, n, f):
                e, p = R * U + n, n % 2
                dve.wait_ge(silu_ready, FC * e + f + 1)
                atleast(dve, y_done, (e - 1) * CT)
                v_.tensor_tensor(act_h[:, p, f, :], act_s[:, f, :], ps[:, 3 + 2 * f, 0:CAP], ALU.mult)\
                    .then_inc(h_ready, 1)

            def z_statistics(e, t, rows, p):
                dve.wait_ge(z_step, e * CT + t + 1)
                v_.bn_stats(zst[0:rows, t, :], z[0:rows, p, t, :]).then_inc(zst_step, 1)

            def combine(R, n):
                e, s, p = R * U + n, n % U, n % 2
                atleast(dve, os_ready, (e - 1) * CT)
                dve.wait_ge(xs_in[s], 32 * (R + n // U + 1))
                for t in range(CT):
                    rows = P if t < CFULL else CREST
                    dve.wait_ge(y_done, e * CT + min(CT, t // 2 * 2 + 2))
                    v_.scalar_tensor_tensor(out=z[0:rows, p, t, :],
                                            in0=ps[0:rows, 6 + t // 2, (t % 2) * D:(t % 2 + 1) * D],
                                            scalar=xs[0:rows, s, t, D:D + 1], in1=xs[0:rows, s, t, 0:D],
                                            op0=ALU.mult, op1=ALU.add).then_inc(z_step, 1)
                    if t > 0:
                        z_statistics(e, t - 1, P, p)
                z_statistics(e, CT - 1, CREST, p)
                atleast(dve, zrs_ready, e - 1, settle=True)
                for t in range(CT):
                    rows = P if t < CFULL else CREST
                    atleast(dve, zst_step, e * CT + t + 1, settle=True)
                    v_.bn_aggr(zmv[0:rows, p, t, :], zst[0:rows, t, :]).then_inc(zmv_ready, 1)

            def turn(R, n, ahead=True):
                hidden(R, n, 0)
                if ahead:
                    low_x(R, n + 1)
                if ahead and n >= 1:
                    low_weights(R, n + 1)
                if n >= 1:
                    combine(R, n - 1)
                hidden(R, n, 1)

            low_x(0, 0)
            turn(0, 0)
            turn(0, 1)
            with dve.Fori(0, (E - 4) // U) as R:
                for n in range(2, 2 + U):
                    turn(R, n)
            RL = (E - 4) // U
            turn(RL, 2)
            turn(RL, 3, ahead=False)
            combine(RL, 3)


_INS = ["L0_attn_x", "L0_attn_bv_q", "L0_attn_bv_k", "L0_attn_bv_v", "L0_ffn_w_router", "L0_ffn_w_gate",
        "L0_ffn_w_up", "L0_ffn_w_down"]
_OUTS = [((4, 2048, 256), "float32")]


def kernel(**inputs):
    import numpy as _np
    import concourse.bacc as _bacc
    from concourse import mybir as _mybir
    from concourse.bass_utils import run_bass_kernel_spmd as _run

    nc = _bacc.Bacc("TRN2", target_bir_lowering=False, num_devices=1)
    arrays, args = {}, []
    for name in _INS:
        a = _np.ascontiguousarray(inputs[name])
        arrays[f"in_{name}_dram"] = a
        args.append(nc.dram_tensor(f"in_{name}_dram", a.shape, _mybir.dt.from_np(a.dtype), kind="ExternalInput").ap())
    for i, (shape, dtype) in enumerate(_OUTS):
        dt = _mybir.dt.from_np(_np.dtype(dtype))
        args.append(nc.dram_tensor(f"out_{i}_dram", shape, dt, kind="ExternalOutput").ap())
    bass_postln_attn_moe_kernel(nc, *args)
    r = _run(nc, [arrays], core_ids=[0])
    got = tuple(r.results[0][f"out_{i}_dram"] for i in range(len(_OUTS)))
    return got[0]
```
